# Optimizing a Trainium2 kernel written in Bass

```python
import numpy as np
import jax
import jax.numpy as jnp

def _softmax(x, axis=-1):
    return jax.nn.softmax(x, axis=axis)

def _gelu(x):
    return jax.nn.gelu(x, approximate=True)

def _silu(x):
    return jax.nn.silu(x)

def _sigmoid(x):
    return jax.nn.sigmoid(x)

def _layernorm(x, axis=-1, eps=1e-05):
    m = jnp.mean(x, axis=axis, keepdims=True)
    v = jnp.var(x, axis=axis, keepdims=True)
    return (x - m) / jnp.sqrt(v + eps)

def _scatter_add(tgt, idx, src, axis=0):
    return tgt.at[idx].add(src)

def _segment_sum(src, seg, n):
    return jax.ops.segment_sum(src, seg, n)
kernel_name = 'mk_gnn_preln_d2_gnn_r8_723199'

def setup_inputs(seed: int=0):
    np.random.seed(seed)
    _w = jnp.asarray

    def _rec_inputs():
        import jax
        import jax.numpy as jnp
        _gk = jax.random.key(seed)
        x = -0.0001006 + 1 * jax.random.normal(jax.random.fold_in(_gk, 1), (12500, 96), jnp.float32)
        src = jax.random.randint(jax.random.fold_in(_gk, 2), (200000,), 0, 12500, jnp.int32)
        dst = jax.random.randint(jax.random.fold_in(_gk, 3), (200000,), 0, 12500, jnp.int32)
        _o = jnp.argsort(dst, stable=True)
        src = src[_o]
        dst = dst[_o]
        edge_attr_96 = 5.93493e-05 + 1.00006 * jax.random.normal(jax.random.fold_in(_gk, 11), (200000, 96), jnp.float32)
        return (x, src, dst, edge_attr_96)
    x, src, dst, edge_attr_96 = _rec_inputs()

    def _L0_gnn_setup():
        import jax, jax.numpy as jnp
        import numpy as np
        N_NODES = 6250
        N_EDGES = 100000
        IN_DIM = 96
        NUM_HEADS = 8
        HEAD_DIM = IN_DIM // NUM_HEADS
        key = jax.random.key(seed)
        ks = jax.random.split(key, 11)
        s = 1.0 / np.sqrt(IN_DIM)
        return {'x': jax.random.normal(ks[0], (N_NODES, IN_DIM), dtype=jnp.float32), 'edge_index': jax.random.randint(ks[1], (2, N_EDGES), 0, N_NODES, dtype=jnp.int64), 'edge_attr': jax.random.normal(ks[2], (N_EDGES, IN_DIM), dtype=jnp.float32), 'Wq': jax.random.normal(ks[3], (IN_DIM, IN_DIM), dtype=jnp.float32) * s, 'bq': jax.random.normal(ks[4], (IN_DIM,), dtype=jnp.float32) * s, 'Wk': jax.random.normal(ks[5], (IN_DIM, IN_DIM), dtype=jnp.float32) * s, 'bk': jax.random.normal(ks[6], (IN_DIM,), dtype=jnp.float32) * s, 'We': jax.random.normal(ks[7], (IN_DIM, IN_DIM), dtype=jnp.float32) * s, 'be': jax.random.normal(ks[8], (IN_DIM,), dtype=jnp.float32) * s, 'Wv': jax.random.normal(ks[9], (IN_DIM, IN_DIM), dtype=jnp.float32) * s, 'bv': jax.random.normal(ks[10], (IN_DIM,), dtype=jnp.float32) * s}
    _L0_gnn_all = _L0_gnn_setup()
    _L0_gnn_in = {k: v for k, v in _L0_gnn_all.items() if k in ('Wq', 'bq', 'Wk', 'bk', 'We', 'be', 'Wv', 'bv')}
    del _L0_gnn_all

    def _L1_gnn_setup():
        import jax, jax.numpy as jnp
        import numpy as np
        BN_EPS = 1e-05
        key = jax.random.key(seed)
        ks = jax.random.split(key, 5)
        N, E, D = (6250, 100000, 96)
        x = jax.random.normal(ks[0], (N, D), dtype=jnp.float32)
        edge_index = jax.random.randint(ks[1], (2, E), 0, N, dtype=jnp.int64)
        Wl = jax.random.normal(ks[2], (D, D), dtype=jnp.float32) / np.sqrt(D)
        bl = jnp.zeros((D,), dtype=jnp.float32)
        Wr = jax.random.normal(ks[3], (D, D), dtype=jnp.float32) / np.sqrt(D)
        gamma = jnp.ones((D,), dtype=jnp.float32)
        beta = jnp.zeros((D,), dtype=jnp.float32)
        return {'x': x, 'edge_index': edge_index, 'Wl': Wl, 'bl': bl, 'Wr': Wr, 'gamma': gamma, 'beta': beta}
    _L1_gnn_all = _L1_gnn_setup()
    _L1_gnn_in = {k: v for k, v in _L1_gnn_all.items() if k in ('Wl', 'bl', 'Wr', 'gamma', 'beta')}
    del _L1_gnn_all
    return {'x': x, 'src': src, 'dst': dst, 'edge_attr_96': edge_attr_96, 'L0_gnn_Wq': _L0_gnn_in['Wq'], 'L0_gnn_bq': _L0_gnn_in['bq'], 'L0_gnn_Wk': _L0_gnn_in['Wk'], 'L0_gnn_bk': _L0_gnn_in['bk'], 'L0_gnn_We': _L0_gnn_in['We'], 'L0_gnn_be': _L0_gnn_in['be'], 'L0_gnn_Wv': _L0_gnn_in['Wv'], 'L0_gnn_bv': _L0_gnn_in['bv'], 'L1_gnn_Wl': _L1_gnn_in['Wl'], 'L1_gnn_bl': _L1_gnn_in['bl'], 'L1_gnn_Wr': _L1_gnn_in['Wr'], 'L1_gnn_gamma': _L1_gnn_in['gamma'], 'L1_gnn_beta': _L1_gnn_in['beta']}

def reference(x, src, dst, edge_attr_96, L0_gnn_Wq, L0_gnn_bq, L0_gnn_Wk, L0_gnn_bk, L0_gnn_We, L0_gnn_be, L0_gnn_Wv, L0_gnn_bv, L1_gnn_Wl, L1_gnn_bl, L1_gnn_Wr, L1_gnn_gamma, L1_gnn_beta):
    import jax
    import jax.numpy as jnp

    def _L0_gnn_ref(x, edge_index, edge_attr, Wq, bq, Wk, bk, We, be, Wv, bv):
        import jax, jax.numpy as jnp
        import numpy as np
        N_NODES = 6250
        N_EDGES = 100000
        IN_DIM = 96
        NUM_HEADS = 8
        HEAD_DIM = IN_DIM // NUM_HEADS
        N = x.shape[0]
        H, D = (NUM_HEADS, HEAD_DIM)
        Q_h = (x @ Wq + bq).reshape(N, H, D)
        K_h = (x @ Wk + bk).reshape(N, H, D)
        V_h = (x @ Wv + bv).reshape(N, H, D)
        E = (edge_attr @ We + be).reshape(-1, H, D)
        src_idx = edge_index[0]
        dst_idx = edge_index[1]
        src = K_h[src_idx]
        dest = Q_h[dst_idx]
        score = src * dest / jnp.sqrt(jnp.asarray(D, x.dtype))
        score = score * E
        score = jnp.exp(jnp.clip(score.sum(-1, keepdims=True), -5.0, 5.0))
        msg = V_h[src_idx] * score
        wV = jax.ops.segment_sum(msg, dst_idx, num_segments=N)
        Z = jax.ops.segment_sum(score, dst_idx, num_segments=N)
        h_out = wV / (Z + 1e-06)
        return h_out.reshape(N, H * D)

    def _L1_gnn_ref(x, edge_index, Wl, bl, Wr, gamma, beta):
        import jax, jax.numpy as jnp
        import numpy as np
        BN_EPS = 1e-05
        N = x.shape[0]
        src, dst = (edge_index[0], edge_index[1])
        msg_sum = jax.ops.segment_sum(x[src], dst, num_segments=N)
        deg = jax.ops.segment_sum(jnp.ones_like(src, dtype=x.dtype), dst, num_segments=N)
        neigh_mean = msg_sum / jnp.maximum(deg, 1.0)[:, None]
        h = jnp.einsum('nd,od->no', neigh_mean, Wl) + bl + jnp.einsum('nd,od->no', x, Wr)
        mu = h.mean(axis=0)
        var = h.var(axis=0)
        h = (h - mu) * jax.lax.rsqrt(var + BN_EPS) * gamma + beta
        return jax.nn.relu(h)
    edge_index = jnp.stack([src, dst])
    h = jnp.maximum(_layernorm(x, axis=-1), 0.0)
    x = x + _L0_gnn_ref(h, edge_index, edge_attr_96, L0_gnn_Wq, L0_gnn_bq, L0_gnn_Wk, L0_gnn_bk, L0_gnn_We, L0_gnn_be, L0_gnn_Wv, L0_gnn_bv)
    h = jnp.maximum(_layernorm(x, axis=-1), 0.0)
    x = x + _L1_gnn_ref(h, edge_index, L1_gnn_Wl, L1_gnn_bl, L1_gnn_Wr, L1_gnn_gamma, L1_gnn_beta)
    return x

_drawn_inputs = setup_inputs


def setup_inputs(seed=0):
    import zlib

    import numpy as np

    out = dict(_drawn_inputs(seed))
    spreads = {'L1_gnn_bl': (0.0, 0.8), 'L1_gnn_gamma': (1.0, 0.2), 'L1_gnn_beta': (0.0, 0.1)}
    factors = {'L0_gnn_bq': 5.029, 'L0_gnn_bk': 4.815, 'L0_gnn_be': 7.062}
    for name, (base, spread) in spreads.items():
        noise = np.random.default_rng([zlib.crc32(name.encode()), seed]).standard_normal(out[name].shape)
        drawn = base * np.exp(spread * noise) if base else spread * noise
        out[name] = jnp.asarray(drawn.astype(out[name].dtype))
    for name, factor in factors.items():
        out[name] = (out[name] * factor).astype(out[name].dtype)
    return out
```

```python
from contextlib import ExitStack

import concourse.bass as bass
from concourse import mybir

F32 = mybir.dt.float32
I32 = mybir.dt.int32
ALU = mybir.AluOpType
ACT = mybir.ActivationFunctionType
AX_X = mybir.AxisListType.X

P = 128
HEADS = 8
WIN = 64
TILES = 4
ROWS = P * TILES
RING = 4
EPS = 1e-5
Z_EPS = 1e-6
CLIP = 5.0


def graph_attention_then_sage_kernel(nc, x, src, dst, edge_attr, Wq, bq, Wk, bk, We, be, Wv, bv,
                                     Wl, bl, Wr, gamma, beta, out):
    N, D = x.shape
    E = src.shape[0]
    DH = D // HEADS
    KV = 2 * D
    MSG = D + HEADS
    NB = -(-(-(-E // ROWS)) // RING) * RING
    G = -(-N // ROWS)
    NT = G * TILES
    NPAD = G * ROWS
    FULL = N // P
    REST = N - FULL * P
    LASTB = NB - RING
    QCH = NB // 4
    assert G % 2 == 1 and NB % 4 == 0 and QCH <= P and N + WIN <= NPAD

    def start_of(b):
        return min(b * ROWS, E - ROWS) if isinstance(b, int) else b * ROWS

    def repeated_partitions(b):
        return min(max(b * ROWS - (E - ROWS), 0), ROWS) // TILES

    kv_tab = nc.dram_tensor("kv_tab", [NPAD, KV], F32, kind="Internal").ap()
    q_tab = nc.dram_tensor("q_tab", [NPAD, D], F32, kind="Internal").ap()
    h1_tab = nc.dram_tensor("h1_tab", [NPAD, D], F32, kind="Internal").ap()

    def node_rows(table, g):
        return table[bass.ds(g * ROWS, ROWS), :].rearrange("(t p) f -> p t f", p=P)

    def edges(vec, b):
        return vec[bass.ds(start_of(b), ROWS)]

    with ExitStack() as ctx:
        def sb(name, shape, dt=F32):
            return ctx.enter_context(nc.sbuf_tensor(name, shape, dt))

        def sem(name):
            return ctx.enter_context(nc.semaphore(name))

        x_sb = sb("x_sb", [P, NT, D])
        h_sb = sb("h_sb", [P, NT, D])
        acc = sb("acc", [MSG, NPAD])
        ident = sb("ident", [P, P])
        ones = sb("ones", [P, P])
        eps = sb("eps", [P, 1])
        iota_w = sb("iota_w", [P, WIN])
        iota_p = sb("iota_p", [P, 1])
        wkv = sb("wkv", [D + 1, KV])
        wq = sb("wq", [D + 1, D])
        we = sb("we", [D + 1, D])
        wl_in = sb("wl_in", [D, D])
        wr_in = sb("wr_in", [D, D])
        wl = sb("wl", [D + 1, D + 1])
        wr = sb("wr", [D + 1, D])
        gamma_b = sb("gamma_b", [P, D])
        beta_b = sb("beta_b", [P, D])
        dst_rel0 = sb("dst_rel0", [P, NB, TILES])
        dst_rel = sb("dst_rel", [P, NB, TILES])
        win_node = sb("win_node", [P, NB])
        base_i = sb("base_i", [1, NB], I32)
        span_i = sb("span_i", [1, 1], I32)
        h_flat = h_sb[:, :, :].rearrange("p t f -> p (t f)")
        SET = NB * TILES
        dst_i = h_flat[:, 0:SET].bitcast(I32).rearrange("p (b t) -> p b t", t=TILES)
        dst_f = h_flat[:, SET:2 * SET].rearrange("p (b t) -> p b t", t=TILES)
        dst_mn = h_flat[:, 2 * SET:2 * SET + NB]
        dst_mx = h_flat[:, 2 * SET + NB:2 * SET + 2 * NB]
        col_mn = h_flat[:, 2 * SET + 2 * NB:2 * SET + 2 * NB + 4]
        col_mx = h_flat[:, 2 * SET + 2 * NB + 4:2 * SET + 2 * NB + 8]
        diag_mn = h_flat[:, 3 * SET:3 * SET + NB]
        diag_mx = h_flat[:, 3 * SET + NB:3 * SET + 2 * NB]
        base_b = h_flat[:, 3 * SET + 2 * NB:3 * SET + 3 * NB]
        span_b = h_flat[:, 3 * SET + 3 * NB:3 * SET + 4 * NB]
        span_m = h_flat[:, 4 * SET:4 * SET + 1]
        iota_pi = h_flat[:, 4 * SET + 1:4 * SET + 2].bitcast(I32)
        iota_i = h_flat[:, 5 * SET:5 * SET + WIN].bitcast(I32)
        kvg = sb("kvg", [P, RING, TILES * KV])
        kv_slot = [kvg[:, k, :].rearrange("p (t f) -> p t f", f=KV) for k in range(RING)]
        h1_slot = [kvg[:, k, 0:TILES * (D + 1)].rearrange("p (t f) -> p t f", f=D + 1) for k in range(RING)]
        idx = sb("idx", [P, RING, TILES], I32)
        ea = sb("ea", [P, RING, TILES, D])
        dst_row = sb("dst_row", [WIN, RING, ROWS], I32)
        q_win = sb("q_win", [WIN, RING, D])
        ea_t = sb("ea_t", [D + 1, 2, ROWS])
        sel = sb("sel", [P, 2, TILES, WIN])
        sel_t = sb("sel_t", [WIN, 2, TILES, P])
        prod = sb("prod", [P, TILES * D])
        score = sb("score", [P, TILES * HEADS])
        msg = sb("msg", [P, 2, TILES, MSG])
        node_sum = sb("node_sum", [P, 2, TILES])
        node_sq = sb("node_sq", [P, 2, TILES])
        centred = sb("centred", [P, 2, TILES, D])
        squares = msg[:, :, :, 0:D]
        normed = sb("normed", [P, 2, TILES, D])
        h_t = sb("h_t", [D + 1, 2, ROWS])
        kv_out = sb("kv_out", [P, 2, TILES, KV])
        q_out = sb("q_out", [P, 2, TILES, D])
        acc_st = kv_out
        rz = sb("rz", [P, 2, TILES * HEADS])
        mean_b = prod[:, 0:D]
        scale_b = prod[:, D:2 * D]

        acc_stage = [acc_st[:, k, :, :].rearrange("p t f -> p (t f)")[:, 0:ROWS] for k in range(2)]

        bank = [ctx.enter_context(nc.psum_tensor(f"bank{i}", [P, 512], F32)) for i in range(8)]
        b_tr, b_e, b_q, b_agg = bank[0:2], bank[2:4], bank[4:6], bank[6:8]

        s_const = sem("s_const")
        s_x = sem("s_x")
        s_dst = sem("s_dst")
        s_idx = [sem(f"s_idx{k}") for k in range(RING)]
        s_ea = [sem(f"s_ea{k}") for k in range(RING)]
        s_dstrow = [sem(f"s_dstrow{k}") for k in range(RING)]
        s_qwin = [sem(f"s_qwin{k}") for k in range(RING)]
        s_kv = [sem(f"s_kv{k}") for k in range(RING)]
        s_idx1 = [sem(f"s_idx1{k}") for k in range(RING)]
        s_h1g = [sem(f"s_h1g{k}") for k in range(RING)]
        s_gate = sem("s_gate")
        s_pool = sem("s_pool")
        s_iota = sem("s_iota")
        s_wt = sem("s_wt")
        s_wt_sb = sem("s_wt_sb")
        s_norm_step = sem("s_norm_step")
        s_win_step = sem("s_win_step")
        s_mid_step = sem("s_mid_step")
        s_lin_step = sem("s_lin_step")
        s_bn_step = sem("s_bn_step")
        s_fin_step = sem("s_fin_step")
        s_sq = sem("s_sq")
        s_std = sem("s_std")
        s_normed = sem("s_normed")
        s_ht_ps = sem("s_ht_ps")
        s_ht = sem("s_ht")
        s_kvq = sem("s_kvq")
        s_stage_v = sem("s_stage_v")
        s_stage_a = sem("s_stage_a")
        s_kvst = [sem(f"s_kvst{k}") for k in range(2)]
        s_qst = [sem(f"s_qst{k}") for k in range(2)]
        s_mn_t = sem("s_mn_t")
        s_diag = sem("s_diag")
        s_bc = sem("s_bc")
        s_base = sem("s_base")
        s_ea_ps = sem("s_ea_ps")
        s_ea_t = sem("s_ea_t")
        s_e = sem("s_e")
        s_q = sem("s_q")
        s_sel_t = sem("s_sel_t")
        s_kq = sem("s_kq")
        s_kqe = sem("s_kqe")
        s_dot = sem("s_dot")
        s_clip = sem("s_clip")
        s_exp = sem("s_exp")
        s_msg = sem("s_msg")
        s_agg = sem("s_agg")
        s_acc = sem("s_acc")
        s_pass = sem("s_pass")
        s_ones_col = sem("s_ones_col")
        s_mst = sem("s_mst")
        s_mt = sem("s_mt")
        s_hout = sem("s_hout")
        s_msq = sem("s_msq")
        s_mstd = sem("s_mstd")
        s_mnormed = sem("s_mnormed")
        s_h1 = sem("s_h1")
        s_h1st = [sem(f"s_h1st{k}") for k in range(2)]
        s_acc0 = sem("s_acc0")
        s_sel1 = sem("s_sel1")
        s_agg1 = sem("s_agg1")
        s_acc1 = sem("s_acc1")
        s_pass1 = sem("s_pass1")
        s_fst = sem("s_fst")
        s_h1ld = [sem(f"s_h1ld{k}") for k in range(2)]
        s_fht_ps = sem("s_fht_ps")
        s_fht = sem("s_fht")
        s_lin = sem("s_lin")
        s_hh = sem("s_hh")
        s_sum = sem("s_sum")
        s_mean = sem("s_mean")
        s_cent = sem("s_cent")
        s_fsq = sem("s_fsq")
        s_var = sem("s_var")
        s_bsq = sem("s_bsq")
        s_bstd = sem("s_bstd")
        s_o = sem("s_o")
        s_out = [sem(f"s_out{k}") for k in range(2)]

        CONSTS = 13
        PADDED, IDENTITY, EPSILON, CORNER, ONE_ROWS, IOTAS, CLEARED = 1, 3, 5, 7, 9, 11, 12
        X_LOADS = 4
        x_load_tiles = FULL // X_LOADS

        def windows(eng):
            eng.wait_ge(s_base, 1)
            return (eng.value_load(span_i[0:1, 0:1], min_val=0, max_val=N - 1) >> 6) + 1

        def base_of(eng, b, w):
            first = eng.value_load(base_i[0:1, bass.ds(b, 1)], min_val=0, max_val=N - 1)
            node = first + w * WIN
            return (node + (node > N) * (N - node)).with_bounds(min_val=0, max_val=N)

        def edge_steps(eng, w, step):
            def one(b, k, j):
                step(b, k, w * NB + b, w * (NB // RING) + j,
                     isinstance(b, int) and b == 0, isinstance(b, int) and b == NB - 1)
            for k in range(RING):
                one(k, k, 0)
            with eng.Fori(1, NB // RING - 1) as j:
                for k in range(RING):
                    one(j * RING + k, k, j)
            for k in range(RING):
                one(LASTB + k, k, NB // RING - 1)

        def node_steps(eng, ahead, behind, after=lambda g, k, j: None):
            ahead(0, 0, 0)
            after(0, 0, 0)
            with eng.Fori(0, G // 2) as j:
                ahead(j * 2 + 1, 1, j)
                behind(j * 2, 0, j)
                after(j * 2 + 1, 1, j)
                ahead(j * 2 + 2, 0, j + 1)
                behind(j * 2 + 1, 1, j)
                after(j * 2 + 2, 0, j + 1)
            behind(G - 1, 0, G // 2)

        def node_steps_apart(eng, one):
            one(0, 0, 0)
            with eng.Fori(0, G // 2 - 1) as j:
                one(j * 2 + 1, 1, j)
                one(j * 2 + 2, 0, j + 1)
            one(G - 2, 1, G // 2 - 1)
            one(G - 1, 0, G // 2)

        block = ctx.enter_context(nc.Block())

        @block.sync
        def _(sp):
            for s, count in ((s_ea_t, 2), (s_e, 2), (s_q, 2), (s_kq, 2), (s_kqe, 2), (s_msg, RING),
                             (s_agg, 2), (s_acc, 2), (s_agg1, RING), (s_acc1, 2), (s_sel1, 2),
                             (s_ht_ps, 2), (s_ht, 2), (s_kvq, 2), (s_stage_v, 2), (s_stage_a, 2),
                             (s_mt, 2), (s_hout, 2), (s_mnormed, 2), (s_h1, 2),
                             (s_fht_ps, 2), (s_fht, 2), (s_lin, 2), (s_hh, 2), (s_fsq, 2), (s_var, 2),
                             (s_kvst[0], 16), (s_kvst[1], 16), (s_qst[0], 16), (s_qst[1], 16),
                             (s_h1st[0], 16), (s_h1st[1], 16), (s_out[0], 16), (s_out[1], 16)):
                sp.sem_inc(s, count)
            for c in range(X_LOADS):
                t0 = c * x_load_tiles
                t1 = FULL if c == X_LOADS - 1 else t0 + x_load_tiles
                sp.dma_start(x_sb[:, t0:t1, :],
                             x[t0 * P:t1 * P, :].rearrange("(t p) f -> p t f", p=P)).then_inc(s_x, 16)
            sp.wait_ge(s_pool, PADDED)
            sp.dma_start(x_sb[0:REST, FULL, :], x[FULL * P:N, :]).then_inc(s_x, 16)
            row = lambda v: v.rearrange("(a d) -> a d", a=1)
            for to, of in ((wkv[0:D, 0:D], Wk), (wkv[0:D, D:KV], Wv), (wkv[D:D + 1, 0:D], row(bk)),
                           (wkv[D:D + 1, D:KV], row(bv)), (wq[0:D, :], Wq), (wq[D:D + 1, :], row(bq)),
                           (we[0:D, :], We), (we[D:D + 1, :], row(be)), (wl_in[:, :], Wl), (wr_in[:, :], Wr),
                           (wr[D:D + 1, :], row(bl)), (gamma_b[:, :], row(gamma).to_broadcast([P, D])),
                           (beta_b[:, :], row(beta).to_broadcast([P, D]))):
                sp.dma_start(to, of).then_inc(s_const, 16)
            whole = E // ROWS
            sp.dma_start(dst_i[:, 0:whole, :],
                         dst[0:whole * ROWS].rearrange("(b p t) -> p b t", p=P, t=TILES)).then_inc(s_dst, 16)
            for b in range(whole, NB):
                sp.dma_start(dst_i[:, b, :],
                             dst[start_of(b):start_of(b) + ROWS].rearrange("(p t) -> p t", t=TILES)).then_inc(s_dst, 16)

            def store_tables(g, k, j):
                sp.wait_ge(s_stage_v, g + 3)
                sp.wait_ge(s_stage_a, g + 3)
                sp.dma_start(node_rows(kv_tab, g), kv_out[:, k, :, :]).then_inc(s_kvst[k], 16)
                sp.dma_start(node_rows(q_tab, g), q_out[:, k, :, :]).then_inc(s_qst[k], 16)
            node_steps(sp, lambda g, k, j: None, store_tables)
            for k in range(2):
                sp.wait_ge(s_qst[k], 16 * ((G + 1 - k) // 2 + 1))

            with sp.Fori(0, windows(sp)) as w:
                def load(b, k, n, turn, first, last):
                    sp.wait_ge(s_msg, n + 1)
                    sp.dma_start(idx[:, k, :], edges(src, b).rearrange("(p t) -> p t", t=TILES)).then_inc(s_idx[k], 16)
                    sp.dma_start(ea[:, k, :, :], edge_attr[bass.ds(start_of(b), ROWS), :]
                                 .rearrange("(p t) f -> p t f", t=TILES)).then_inc(s_ea[k], 16)
                    sp.dma_start(dst_row[:, k, :], edges(dst, b).rearrange("(a e) -> a e", a=1)
                                 .to_broadcast([WIN, ROWS])).then_inc(s_dstrow[k], 16)
                    sp.dma_start(q_win[:, k, :], q_tab[bass.ds(base_of(sp, b, w), WIN), :]).then_inc(s_qwin[k], 16)
                edge_steps(sp, w, load)

            def store_h1(g, k, j):
                sp.wait_ge(s_h1, g + 3)
                sp.dma_start(node_rows(h1_tab, g), q_out[:, k, :, :]).then_inc(s_h1st[k], 16)
            node_steps(sp, lambda g, k, j: None, store_h1)

            with sp.Fori(0, windows(sp)) as w:
                def load1(b, k, n, turn, first, last):
                    sp.wait_ge(s_agg1, n + 1)
                    sp.dma_start(idx[:, k, :], edges(src, b).rearrange("(p t) -> p t", t=TILES)).then_inc(s_idx1[k], 16)
                edge_steps(sp, w, load1)

            def load_h1(g, k, j):
                sp.wait_ge(s_fht_ps, g + 1)
                sp.dma_start(normed[:, k, :, :], node_rows(h1_tab, g)).then_inc(s_h1ld[k], 16)
            for k in range(2):
                sp.wait_ge(s_h1st[k], 16 * ((G + 1 - k) // 2 + 1))
            node_steps(sp, load_h1, lambda g, k, j: None)

            def store_out(g, k, j):
                sp.wait_ge(s_o, g + 1)
                if isinstance(g, int) and g == G - 1:
                    for t in range(TILES):
                        rows = min(max(N - g * ROWS - t * P, 0), P)
                        if rows:
                            at = g * ROWS + t * P
                            sp.dma_start(out[at:at + rows, :], centred[0:rows, k, t, :]).then_inc(s_out[k], 16)
                else:
                    sp.dma_start(node_rows(out, g), centred[:, k, :, :]).then_inc(s_out[k], 16)
            node_steps_apart(sp, store_out)
            last_stores = -(-(N - (G - 1) * ROWS) // P)
            sp.wait_ge(s_out[0], 16 * (1 + G // 2 + last_stores))
            sp.wait_ge(s_out[1], 16 * (1 + G // 2))

        @block.gpsimd
        def _(pool):
            def made(ins, count=[0]):
                ins.then_inc(s_pool, 1)
                count[0] += 1
                pool.wait_ge(s_pool, count[0])

            made(pool.memset(x_sb[:, FULL:NT, :], 0.0))
            made(pool.memset(ident[:, :], 0.0))
            made(pool.affine_select(out=ident[:, :], in_=ident[:, :], compare_op=ALU.not_equal, fill=1.0, base=0,
                                    pattern=[[-1, P]], channel_multiplier=1))
            made(pool.memset(ones[:, :], 1.0))
            made(pool.memset(eps[:, :], EPS))
            made(pool.memset(wl[:, :], 0.0))
            made(pool.memset(wl[D:D + 1, D:D + 1], 1.0))
            made(pool.memset(h_t[D:D + 1, :, :], 1.0))
            made(pool.memset(ea_t[D:D + 1, :, :], 1.0))
            made(pool.iota(iota_i[:, :], pattern=[[1, WIN]], base=0, channel_multiplier=0))
            made(pool.iota(iota_pi[:, :], pattern=[[0, 1]], base=0, channel_multiplier=1))
            made(pool.memset(acc[:, :], 0.0))

            for k in range(2):
                pool.wait_ge(s_kvst[k], 16 * ((G + 1 - k) // 2 + 1))
            with pool.Fori(0, windows(pool)) as w:
                def gather(b, k, n, turn, first, last):
                    pool.wait_ge(s_idx[k], (turn + 1) * 16)
                    pool.sem_inc(s_gate, 1)
                    for t in range(TILES):
                        pool.indirect_dma_start(
                            out=kv_slot[k][:, t, :], out_offset=None, in_=kv_tab[:, :],
                            in_offset=bass.IndirectOffsetOnAxis(ap=idx[:, k, t:t + 1], axis=0)).then_inc(s_kv[k], 16)
                edge_steps(pool, w, gather)

            pool.wait_ge(s_acc0, 1)
            for k in range(RING):
                pool.memset(h1_slot[k][:, :, D:D + 1], 1.0).then_inc(s_ones_col, 1)
                pool.wait_ge(s_ones_col, k + 1)

            def stage(g, k, j):
                pool.wait_ge(s_mt, g + 1)
                pool.sem_inc(s_gate, 1)
                pool.tensor_copy(acc_stage[k][0:MSG, :], acc[:, bass.ds(g * ROWS, ROWS)]).then_inc(s_mst, 1)
            node_steps(pool, stage, lambda g, k, j: None)
            pool.wait_ge(s_mst, G)
            made(pool.memset(acc[0:D + 1, :], 0.0))

            for k in range(2):
                pool.wait_ge(s_h1st[k], 16 * ((G + 1 - k) // 2 + 1))
            with pool.Fori(0, windows(pool)) as w:
                def gather1(b, k, n, turn, first, last):
                    pool.wait_ge(s_idx1[k], (turn + 1) * 16)
                    pool.sem_inc(s_gate, 1)
                    for t in range(TILES):
                        pool.indirect_dma_start(
                            out=h1_slot[k][:, t, 0:D], out_offset=None, in_=h1_tab[:, :],
                            in_offset=bass.IndirectOffsetOnAxis(ap=idx[:, k, t:t + 1], axis=0)).then_inc(s_h1g[k], 16)
                edge_steps(pool, w, gather1)

            pool.wait_ge(s_acc0, 2)

            def stage1(g, k, j):
                pool.wait_ge(s_lin, g + 1)
                pool.sem_inc(s_gate, 1)
                pool.tensor_copy(acc_stage[k][0:D + 1, :], acc[0:D + 1, bass.ds(g * ROWS, ROWS)]).then_inc(s_fst, 1)
            node_steps(pool, stage1, lambda g, k, j: None)

        @block.tensor
        def _(pe):
            pe.wait_ge(s_pool, IDENTITY)
            pe.wait_ge(s_const, 16 * CONSTS)
            pe.transpose(bank[6][0:D, 0:D], wl_in[:, :], ident[0:D, 0:D])
            pe.transpose(bank[6][0:D, P:P + D], wr_in[:, :], ident[0:D, 0:D]).then_inc(s_wt, 1)
            pe.wait_ge(s_pool, ONE_ROWS)

            def turn_normed(g, k, j):
                pe.wait_ge(s_normed, g + 1)
                pe.wait_ge(s_ht, g + 1)
                for t in range(TILES):
                    mm = pe.transpose(b_tr[k][0:D, t * P:(t + 1) * P], normed[:, k, t, :], ident[:, :])
                mm.then_inc(s_ht_ps, 1)

            def project(g, k, j):
                pe.wait_ge(s_ht, g + 3)
                pe.wait_ge(s_stage_v, g + 1)
                pe.wait_ge(s_stage_a, g + 1)
                for t in range(TILES):
                    rows = h_t[:, k, t * P:(t + 1) * P]
                    pe.matmul(bank[2 + 2 * k + t // 2][:, t % 2 * KV:(t % 2 + 1) * KV], rows, wkv[:, :],
                              start=True, stop=True)
                    mm = pe.matmul(b_agg[k][:, t * D:(t + 1) * D], rows, wq[:, :], start=True, stop=True)
                mm.then_inc(s_kvq, 1)
            pe.wait_ge(s_wt_sb, 1)
            node_steps(pe, lambda g, k, j: None, project, turn_normed)

            pe.wait_ge(s_mn_t, 1)
            pe.wait_ge(s_stage_v, G + 2)
            pe.wait_ge(s_stage_a, G + 2)
            for c in range(4):
                pe.transpose(bank[0][0:QCH, c * P:(c + 1) * P], dst_mn[:, c * QCH:(c + 1) * QCH], ident[:, :])
                mm = pe.transpose(bank[1][0:QCH, c * P:(c + 1) * P], dst_mx[:, c * QCH:(c + 1) * QCH], ident[:, :])
            mm.then_inc(s_mn_t, 1)
            pe.wait_ge(s_diag, 8)
            for c in range(4):
                pe.matmul(bank[2][:, c * QCH:(c + 1) * QCH], ones[0:QCH, :], diag_mn[0:QCH, c * QCH:(c + 1) * QCH],
                          start=True, stop=True)
                mm = pe.matmul(bank[3][:, c * QCH:(c + 1) * QCH], ones[0:QCH, :], diag_mx[0:QCH, c * QCH:(c + 1) * QCH],
                               start=True, stop=True)
            mm.then_inc(s_bc, 1)

            with pe.Fori(0, windows(pe)) as w:
                def turn_ea(k, n, turn):
                    pe.wait_ge(s_ea[k], (turn + 1) * 16)
                    pe.wait_ge(s_ea_t, n + 1)
                    for t in range(TILES):
                        mm = pe.transpose(b_tr[k % 2][0:D, t * P:(t + 1) * P], ea[:, k, t, :], ident[:, :])
                    mm.then_inc(s_ea_ps, 1)

                def aggregate(k, n):
                    pe.wait_ge(s_msg, n + 1 + RING)
                    pe.wait_ge(s_acc, n + 1)
                    for t in range(TILES):
                        mm = pe.matmul(b_agg[k % 2][0:MSG, 0:WIN], msg[:, k % 2, t, :], sel[:, k % 2, t, :],
                                       start=(t == 0), stop=(t == TILES - 1))
                    mm.then_inc(s_agg, 1)

                def step(b, k, n, turn, first, last):
                    if first:
                        turn_ea(k, n, turn)
                    if not last:
                        turn_ea((k + 1) % RING, n + 1, turn + (k + 1) // RING)
                    pe.wait_ge(s_ea_t, n + 3)
                    pe.wait_ge(s_kqe, n + 1)
                    for t in range(TILES):
                        mm = pe.matmul(b_e[k % 2][:, t * D:(t + 1) * D], ea_t[:, k % 2, t * P:(t + 1) * P], we[:, :],
                                       start=True, stop=True)
                    mm.then_inc(s_e, 1)
                    pe.wait_ge(s_qwin[k], (turn + 1) * 16)
                    pe.wait_ge(s_sel_t, n + 1)
                    pe.wait_ge(s_kq, n + 1)
                    for t in range(TILES):
                        mm = pe.matmul(b_q[k % 2][:, t * D:(t + 1) * D], sel_t[:, k % 2, t, :], q_win[:, k, :],
                                       start=True, stop=True)
                    mm.then_inc(s_q, 1)
                    if not first:
                        aggregate((k - 1) % RING, n - 1)
                    if last:
                        aggregate(k, n)
                edge_steps(pe, w, step)

            def turn_sums(g, k, j):
                pe.wait_ge(s_mst, g + 1)
                pe.wait_ge(s_hout, g + 1)
                for t in range(TILES):
                    mm = pe.transpose(bank[k][:, t * MSG:(t + 1) * MSG], acc_stage[k][0:MSG, t * P:(t + 1) * P],
                                      ident[0:MSG, 0:MSG])
                mm.then_inc(s_mt, 1)
            node_steps(pe, turn_sums, lambda g, k, j: None)

            pe.wait_ge(s_ones_col, RING)
            with pe.Fori(0, windows(pe)) as w:
                def step1(b, k, n, turn, first, last):
                    pe.wait_ge(s_h1g[k], (turn + 1) * 16 * TILES)
                    pe.wait_ge(s_sel1, n + 3)
                    pe.wait_ge(s_acc1, n + 1)
                    for t in range(TILES):
                        mm = pe.matmul(b_agg[k % 2][0:D + 1, 0:WIN], h1_slot[k][:, t, :], sel[:, k % 2, t, :],
                                       start=(t == 0), stop=(t == TILES - 1))
                    mm.then_inc(s_agg1, 1)
                edge_steps(pe, w, step1)

            def turn_h1(g, k, j):
                pe.wait_ge(s_h1ld[k], (j + 1) * 16)
                pe.wait_ge(s_fht, g + 1)
                for t in range(TILES):
                    mm = pe.transpose(b_tr[k][0:D, t * P:(t + 1) * P], normed[:, k, t, :], ident[:, :])
                mm.then_inc(s_fht_ps, 1)

            def column_sums(where, rows, g):
                if isinstance(g, int) and g == G - 1:
                    for t in range(TILES):
                        valid = min(max(N - g * ROWS - t * P, 0), P)
                        if valid:
                            mm = pe.matmul(where[:, t * D:(t + 1) * D], ones[0:valid, :], rows(t)[0:valid, :],
                                           start=False, stop=True, skip_group_check=True)
                    return mm
                return pe.matmul(where[:, 0:TILES * D], ones[:, :], rows(None), start=isinstance(g, int) and g == 0,
                                 stop=False, skip_group_check=True)

            def products(g, k, j):
                pe.wait_ge(s_fst, g + 1)
                pe.wait_ge(s_fht, g + 3)
                pe.wait_ge(s_hh, g + 1)
                for t in range(TILES):
                    pe.matmul(b_e[k][:, t * (D + 1):(t + 1) * (D + 1)], acc_stage[k][0:D + 1, t * P:(t + 1) * P],
                              wl[:, :], start=True, stop=True)
                    mm = pe.matmul(b_q[k][:, t * D:(t + 1) * D], h_t[:, k, t * P:(t + 1) * P], wr[:, :],
                                   start=True, stop=True)
                mm.then_inc(s_lin, 1)

            node_steps(pe, turn_h1, products)

            def sum_h(g, k, j):
                pe.wait_ge(s_hh, g + 3)
                def rows(t):
                    at = h_sb[:, bass.ds(g * TILES, TILES), :].rearrange("p t f -> p (t f)")
                    return at if t is None else at[:, t * D:(t + 1) * D]
                mm = column_sums(bank[6], rows, g)
                mm.then_inc(s_sum, 1)
            node_steps_apart(pe, sum_h)

            def sum_sq(g, k, j):
                pe.wait_ge(s_fsq, g + 3)
                mm = column_sums(bank[7], lambda t: squares[:, k, :, :] if t is None else squares[:, k, t, :], g)
                mm.then_inc(s_var, 1)
            node_steps_apart(pe, sum_sq)

        @block.scalar
        def _(act):
            def deviation(k, s_from, s_to, g):
                act.wait_ge(s_from, g + 1)
                nc.scalar.activation(node_sq[:, k, :], node_sq[:, k, :], ACT.Sqrt, bias=eps[:, 0:1],
                                     scale=1.0 / D).then_inc(s_to, 1)

            act.wait_ge(s_pool, EPSILON)

            def turned(g, k, j):
                deviation(k, s_sq, s_std, g)
                act.wait_ge(s_ht_ps, g + 3)
                act.wait_ge(s_kvq, g + 1)
                nc.scalar.activation(h_t[0:D, k, :], b_tr[k][0:D, :], ACT.Relu).then_inc(s_ht, 1)

            def staged(g, k, j):
                act.wait_ge(s_kvq, g + 3)
                act.wait_ge(s_kvst[k], (j + 1) * 16)
                act.wait_ge(s_qst[k], (j + 1) * 16)
                nc.scalar.copy(kv_out[:, k, 2:4, :].rearrange("p t f -> p (t f)"), bank[3 + 2 * k][:, 0:2 * KV])
                nc.scalar.mul(q_out[:, k, :, :].rearrange("p t f -> p (t f)"), b_agg[k][:, 0:TILES * D],
                              float(DH) ** -0.5).then_inc(s_stage_a, 1)
            node_steps(act, turned, staged)

            with act.Fori(0, windows(act)) as w:
                def copy_ea(k, n):
                    act.wait_ge(s_ea_ps, n + 1)
                    act.wait_ge(s_e, n + 1)
                    nc.scalar.copy(ea_t[0:D, k % 2, :], b_tr[k % 2][0:D, :]).then_inc(s_ea_t, 1)

                def step(b, k, n, turn, first, last):
                    if first:
                        copy_ea(k, n)
                    if not last:
                        copy_ea((k + 1) % RING, n + 1)
                    act.wait_ge(s_clip, n + 1)
                    act.wait_ge(s_agg, n + 1)
                    nc.scalar.activation(msg[:, k % 2, :, D:MSG], score[:, :].rearrange("p (t h) -> p t h", h=HEADS),
                                         ACT.Exp).then_inc(s_exp, 1)
                edge_steps(act, w, step)

            def relu(g, k, j):
                act.wait_ge(s_mnormed, g + 3)
                act.wait_ge(s_h1st[k], (j + 1) * 16)
                nc.scalar.activation(q_out[:, k, :, :], normed[:, k, :, :], ACT.Relu).then_inc(s_h1, 1)
            node_steps(act, lambda g, k, j: deviation(k, s_msq, s_mstd, g), relu)

            def turned1(g, k, j):
                act.wait_ge(s_fht_ps, g + 3)
                act.wait_ge(s_lin, g + 1)
                nc.scalar.copy(h_t[0:D, k, :], b_tr[k][0:D, :]).then_inc(s_fht, 1)
            node_steps(act, turned1, lambda g, k, j: None)

            def square(g, k, j):
                act.wait_ge(s_var, g + 1)
                act.wait_ge(s_cent, g + 1)
                act.sem_inc(s_gate, 1)
                nc.scalar.activation(squares[:, k, :, :], h_sb[:, bass.ds(g * TILES, TILES), :],
                                     ACT.Square).then_inc(s_fsq, 1)
            node_steps_apart(act, square)
            act.wait_ge(s_bsq, 1)
            nc.scalar.activation(scale_b, scale_b, ACT.Sqrt, bias=eps[:, 0:1], scale=1.0 / N).then_inc(s_bstd, 1)

        @block.vector
        def _(dve):
            def per_node(v):
                return v.unsqueeze(2).to_broadcast([P, TILES, D])

            def spread(rows, k, own_step, done):
                own_step(nc.vector.reduce_sum(node_sum[:, k, :], rows, AX_X))
                own_step(nc.vector.tensor_scalar(node_sum[:, k, :], node_sum[:, k, :], -1.0 / D, None, ALU.mult))
                own_step(nc.vector.tensor_tensor(centred[:, k, :, :], rows, per_node(node_sum[:, k, :]), ALU.add))
                own_step(nc.vector.tensor_tensor(squares[:, k, :, :], centred[:, k, :, :], centred[:, k, :, :], ALU.mult))
                nc.vector.reduce_sum(node_sq[:, k, :], squares[:, k, :, :], AX_X).then_inc(done, 1)

            def scale(k, own_step, done):
                own_step(nc.vector.reciprocal(node_sum[:, k, :], node_sq[:, k, :]))
                nc.vector.tensor_tensor(normed[:, k, :, :], centred[:, k, :, :], per_node(node_sum[:, k, :]),
                                        ALU.mult).then_inc(done, 1)
            SPREAD_STEPS = 4
            NORM_STEPS = SPREAD_STEPS + 1

            def counted(s_step, before):
                count = [0]

                def step(ins):
                    count[0] += 1
                    ins.then_inc(s_step, 1)
                    dve.wait_ge(s_step, before + count[0])
                return step

            dve.wait_ge(s_pool, IOTAS)
            nc.vector.tensor_copy(iota_w[:, :], iota_i[:, :])
            nc.vector.tensor_copy(iota_p[:, :], iota_pi[:, :]).then_inc(s_iota, 1)
            dve.wait_ge(s_wt, 1)
            dve.wait_ge(s_pool, CORNER)
            nc.vector.tensor_copy(wl[0:D, 0:D], bank[6][0:D, 0:D])
            nc.vector.tensor_copy(wr[0:D, :], bank[6][0:D, P:P + D]).then_inc(s_wt_sb, 1)

            dve.wait_ge(s_x, 16 * (X_LOADS + 1))

            def norm_x(g, k, j):
                dve.wait_ge(s_ht_ps, g + 1)
                dve.sem_inc(s_gate, 1)
                spread(x_sb[:, bass.ds(g * TILES, TILES), :], k, counted(s_norm_step, g * NORM_STEPS), s_sq)

            def scale_x(g, k, j):
                dve.wait_ge(s_std, g + 1)
                scale(k, counted(s_norm_step, g * NORM_STEPS + SPREAD_STEPS), s_normed)

            def stage_kv(g, k, j):
                dve.wait_ge(s_kvq, g + 3)
                dve.wait_ge(s_kvst[k], (j + 1) * 16)
                nc.vector.tensor_copy(kv_out[:, k, 0:2, :].rearrange("p t f -> p (t f)"),
                                      bank[2 + 2 * k][:, 0:2 * KV]).then_inc(s_stage_v, 1)
            node_steps(dve, norm_x, stage_kv, scale_x)

            step = counted(s_win_step, 0)
            dve.wait_ge(s_dst, 16 * (1 + NB - E // ROWS))
            dve.wait_ge(s_iota, 1)
            step(nc.vector.tensor_copy(dst_f, dst_i))
            nc.vector.tensor_reduce(dst_mn, dst_f, AX_X, ALU.min)
            nc.vector.tensor_reduce(dst_mx, dst_f, AX_X, ALU.max).then_inc(s_mn_t, 1)
            dve.wait_ge(s_mn_t, 2)
            step(nc.vector.tensor_reduce(col_mn[0:QCH, :], bank[0][0:QCH, :].rearrange("p (c q) -> p c q", q=P),
                                         AX_X, ALU.min))
            step(nc.vector.tensor_reduce(col_mx[0:QCH, :], bank[1][0:QCH, :].rearrange("p (c q) -> p c q", q=P),
                                         AX_X, ALU.max))
            for c in range(4):
                for diag, col in ((diag_mn, col_mn), (diag_mx, col_mx)):
                    nc.vector.tensor_scalar(diag[0:QCH, c * QCH:(c + 1) * QCH], ident[0:QCH, 0:QCH], col[0:QCH, c:c + 1],
                                            None, ALU.mult).then_inc(s_diag, 1)
            dve.wait_ge(s_bc, 1)
            step(nc.vector.tensor_copy(base_b, bank[2][:, 0:NB]))
            step(nc.vector.tensor_tensor(span_b, bank[3][:, 0:NB], base_b, ALU.subtract))
            step(nc.vector.tensor_reduce(span_m, span_b, AX_X, ALU.max))
            step(nc.vector.tensor_copy(span_i[0:1, :], span_m[0:1, :]))
            step(nc.vector.tensor_copy(base_i[0:1, :], base_b[0:1, :]))
            step(nc.vector.tensor_scalar(win_node[:, :], base_b, iota_p[:, 0:1], -float(WIN), ALU.add, ALU.add))
            step(nc.vector.tensor_tensor(dst_rel0[:, :, :], dst_f,
                                         base_b.unsqueeze(2).to_broadcast([P, NB, TILES]), ALU.subtract))
            step(nc.vector.tensor_scalar(dst_rel0[:, :, :], dst_rel0[:, :, :], float(WIN), None, ALU.add))
            for b in range(E // ROWS, NB):
                rep = repeated_partitions(b)
                if rep:
                    step(nc.vector.memset(dst_rel0[0:rep, b, :], -1.0))
            step(nc.vector.tensor_copy(dst_rel[:, :, :], dst_rel0[:, :, :]))
            nc.vector.tensor_copy(span_i[0:1, :], span_m[0:1, :]).then_inc(s_base, 1)

            def move_windows(done, w, turned):
                nc.vector.tensor_scalar(dst_rel[:, :, :], dst_rel[:, :, :], float(WIN), None,
                                        ALU.subtract).then_inc(done, 1)
                if turned:
                    nc.vector.tensor_scalar(win_node[:, :], win_node[:, :], float(WIN), None,
                                            ALU.add).then_inc(done, 1)
                dve.wait_ge(done, (w + 1) * (2 if turned else 1))

            def select(b, k):
                return nc.vector.tensor_tensor(
                    sel[:, k % 2, :, :], iota_w[:, :].unsqueeze(1).to_broadcast([P, TILES, WIN]),
                    dst_rel[:, bass.ds(b, 1), :].rearrange("p a t -> p (a t)").unsqueeze(2).to_broadcast([P, TILES, WIN]),
                    ALU.is_equal)

            def add_sums(b, k, w, n, rows, s_from, credit, s_done):
                at = acc[0:rows, bass.ds(base_of(dve, b, w), WIN)]
                dve.wait_ge(s_from, n + 1 + credit)
                dve.wait_ge(s_done, n + 2)
                dve.sem_inc(s_gate, 1)
                nc.vector.tensor_tensor(at, at, b_agg[k % 2][0:rows, 0:WIN], ALU.add).then_inc(s_done, 1)

            dve.wait_ge(s_pool, CLEARED)
            with dve.Fori(0, windows(dve)) as w:
                move_windows(s_pass, w, True)

                def select_t(b, k, n, turn):
                    dve.wait_ge(s_dstrow[k], (turn + 1) * 16)
                    dve.wait_ge(s_q, n + 1)
                    dve.sem_inc(s_gate, 1)
                    nc.vector.tensor_scalar(sel_t[:, k % 2, :, :], dst_row[:, k, :].rearrange("w (p t) -> w t p", t=TILES),
                                            win_node[0:WIN, bass.ds(b, 1)], None, ALU.is_equal).then_inc(s_sel_t, 1)

                def step(b, k, n, turn, first, last):
                    if first:
                        select_t(b, k, n, turn)
                    heads = lambda v: v.rearrange("p t (h d) -> p t h d", h=HEADS)
                    p3 = prod[:, :].rearrange("p (t f) -> p t f", f=D)
                    dve.wait_ge(s_kv[k], (turn + 1) * 16 * TILES)
                    dve.wait_ge(s_q, n + 3)
                    nc.vector.tensor_tensor(p3, kv_slot[k][:, :, 0:D], b_q[k % 2][:, 0:TILES * D]
                                            .rearrange("p (t f) -> p t f", f=D), ALU.mult).then_inc(s_kq, 1)
                    if not last:
                        select_t(b + 1, (k + 1) % RING, n + 1, turn + (k + 1) // RING)
                    dve.wait_ge(s_e, n + 3)
                    dve.wait_ge(s_kq, n + 3)
                    nc.vector.tensor_tensor(prod[:, :], prod[:, :], b_e[k % 2][:, 0:TILES * D], ALU.mult).then_inc(s_kqe, 1)
                    dve.wait_ge(s_agg, n + 1)
                    dve.sem_inc(s_gate, 1)
                    select(b, k)
                    dve.wait_ge(s_kqe, n + 3)
                    nc.vector.reduce_sum(score[:, :], prod[:, :].rearrange("p (g d) -> p g d", d=DH), AX_X).then_inc(s_dot, 1)
                    if not first:
                        add_sums(b - 1, (k - 1) % RING, w, n - 1, MSG, s_agg, 2, s_acc)
                    dve.wait_ge(s_dot, n + 1)
                    nc.vector.tensor_scalar(score[:, :], score[:, :], -CLIP, CLIP, ALU.max, ALU.min).then_inc(s_clip, 1)
                    dve.wait_ge(s_exp, n + 1)
                    nc.vector.tensor_tensor(heads(msg[:, k % 2, :, 0:D]), heads(kv_slot[k][:, :, D:KV]),
                                            msg[:, k % 2, :, D:MSG].unsqueeze(3).to_broadcast([P, TILES, HEADS, DH]),
                                            ALU.mult).then_inc(s_msg, 1)
                    if last:
                        add_sums(b, k, w, n, MSG, s_agg, 2, s_acc)
                edge_steps(dve, w, step)
            passes = windows(dve)
            dve.wait_ge(s_acc, passes * NB + 2)
            nc.vector.tensor_copy(dst_rel[:, :, :], dst_rel0[:, :, :]).then_inc(s_acc0, 1)

            SUM_STEPS = 3

            def first_layer(g, k, j):
                own_step = counted(s_mid_step, g * (NORM_STEPS + SUM_STEPS))
                sums = bank[k][:, 0:TILES * MSG].rearrange("p (t f) -> p t f", f=MSG)
                z = rz[:, k, :].rearrange("p (t h) -> p t h", h=HEADS)
                rows = x_sb[:, bass.ds(g * TILES, TILES), :]
                heads = lambda v: v.rearrange("p t (h d) -> p t h d", h=HEADS)
                dve.wait_ge(s_mt, g + 3)
                own_step(nc.vector.tensor_scalar(z, sums[:, :, D:MSG], Z_EPS, None, ALU.add))
                own_step(nc.vector.reciprocal(z, z))
                nc.vector.tensor_tensor(heads(centred[:, k, :, :]), heads(sums[:, :, 0:D]),
                                        z.unsqueeze(3).to_broadcast([P, TILES, HEADS, DH]), ALU.mult).then_inc(s_hout, 1)
                dve.wait_ge(s_hout, g + 3)
                dve.sem_inc(s_gate, 1)
                own_step(nc.vector.tensor_tensor(rows, rows, centred[:, k, :, :], ALU.add))
                dve.sem_inc(s_gate, 1)
                spread(rows, k, own_step, s_msq)

            def scale_first(g, k, j):
                dve.wait_ge(s_mstd, g + 1)
                dve.wait_ge(s_h1, g + 1)
                scale(k, counted(s_mid_step, g * (NORM_STEPS + SUM_STEPS) + SUM_STEPS + SPREAD_STEPS), s_mnormed)
            node_steps(dve, first_layer, lambda g, k, j: None, scale_first)

            dve.wait_ge(s_pool, CLEARED + 1)
            with dve.Fori(0, passes) as w:
                move_windows(s_pass1, w, False)

                def step1(b, k, n, turn, first, last):
                    dve.wait_ge(s_agg1, n + 3)
                    dve.sem_inc(s_gate, 1)
                    select(b, k).then_inc(s_sel1, 1)
                    if not first:
                        add_sums(b - 1, (k - 1) % RING, w, n - 1, D + 1, s_agg1, RING, s_acc1)
                    if last:
                        add_sums(b, k, w, n, D + 1, s_agg1, RING, s_acc1)
                edge_steps(dve, w, step1)
            dve.wait_ge(s_acc1, passes * NB + 2)
            nc.vector.memset(rz[:, :, :], 0.0).then_inc(s_acc0, 1)

            LIN_STEPS = 3

            def second_layer(g, k, j):
                own_step = counted(s_lin_step, g * LIN_STEPS)
                lin = b_e[k][:, 0:TILES * (D + 1)].rearrange("p (t f) -> p t f", f=D + 1)
                dve.wait_ge(s_lin, g + 3)
                dve.sem_inc(s_gate, 1)
                own_step(nc.vector.tensor_scalar(node_sum[:, k, :].unsqueeze(2), lin[:, :, D:D + 1], 1.0, None, ALU.max))
                own_step(nc.vector.reciprocal(node_sum[:, k, :], node_sum[:, k, :]))
                own_step(nc.vector.tensor_tensor(centred[:, k, :, :], lin[:, :, 0:D], per_node(node_sum[:, k, :]), ALU.mult))
                nc.vector.tensor_tensor(h_sb[:, bass.ds(g * TILES, TILES), :], centred[:, k, :, :],
                                        b_q[k][:, 0:TILES * D].rearrange("p (t f) -> p t f", f=D),
                                        ALU.add).then_inc(s_hh, 1)
            node_steps(dve, second_layer, lambda g, k, j: None)

            def per_feature(v):
                return v.unsqueeze(1).to_broadcast([P, TILES, D])

            def over_tiles(sums):
                return sums[:, 0:TILES * D].rearrange("p (t f) -> p f t", f=D)

            step = counted(s_bn_step, 0)
            dve.wait_ge(s_sum, G)
            step(nc.vector.reduce_sum(mean_b[:, :], over_tiles(bank[6]), AX_X))
            step(nc.vector.tensor_scalar(mean_b[:, :], mean_b[:, :], 1.0 / N, None, ALU.mult))

            def centre(g, k, j):
                rows = h_sb[:, bass.ds(g * TILES, TILES), :]
                nc.vector.tensor_tensor(rows, rows, per_feature(mean_b[:, :]), ALU.subtract).then_inc(s_cent, 1)
            node_steps_apart(dve, centre)
            dve.wait_ge(s_cent, G)
            dve.wait_ge(s_const, 16 * CONSTS)
            dve.wait_ge(s_var, G + 2)
            nc.vector.reduce_sum(scale_b[:, :], over_tiles(bank[7]), AX_X).then_inc(s_bsq, 1)
            dve.wait_ge(s_bstd, 1)
            step(nc.vector.reciprocal(scale_b[:, :], scale_b[:, :]))
            step(nc.vector.tensor_tensor(scale_b[:, :], scale_b[:, :], gamma_b[:, :], ALU.mult))

            FIN_STEPS = 2

            def finish(g, k, j):
                own_step = counted(s_fin_step, g * FIN_STEPS)
                rows = bass.ds(g * TILES, TILES)
                dve.wait_ge(s_out[k], (j + 1) * 16)
                dve.sem_inc(s_gate, 1)
                own_step(nc.vector.tensor_tensor(centred[:, k, :, :], h_sb[:, rows, :], per_feature(scale_b[:, :]), ALU.mult))
                own_step(nc.vector.tensor_tensor(centred[:, k, :, :], centred[:, k, :, :], per_feature(beta_b[:, :]), ALU.add))
                nc.vector.scalar_tensor_tensor(out=centred[:, k, :, :], in0=centred[:, k, :, :], scalar=0.0,
                                               in1=x_sb[:, rows, :], op0=ALU.max, op1=ALU.add).then_inc(s_o, 1)
            node_steps_apart(dve, finish)


_INS = ['x', 'src', 'dst', 'edge_attr_96', 'L0_gnn_Wq', 'L0_gnn_bq', 'L0_gnn_Wk', 'L0_gnn_bk', 'L0_gnn_We', 'L0_gnn_be',
        'L0_gnn_Wv', 'L0_gnn_bv', 'L1_gnn_Wl', 'L1_gnn_bl', 'L1_gnn_Wr', 'L1_gnn_gamma', 'L1_gnn_beta']


def kernel(**inputs):
    import numpy as _np
    import concourse.bacc as _bacc
    from concourse import mybir as _mybir
    from concourse.bass_utils import run_bass_kernel_spmd as _run

    nc = _bacc.Bacc("TRN2", target_bir_lowering=False, num_devices=1)
    arrays, args = {}, []
    for name in _INS:
        a = _np.ascontiguousarray(inputs[name])
        arrays[f"in_{name}_dram"] = a
        args.append(nc.dram_tensor(f"in_{name}_dram", a.shape, _mybir.dt.from_np(a.dtype), kind="ExternalInput").ap())
    out = nc.dram_tensor("out_0_dram", arrays["in_x_dram"].shape, _mybir.dt.float32, kind="ExternalOutput").ap()
    graph_attention_then_sage_kernel(nc, *args, out)
    r = _run(nc, [arrays], core_ids=[0])
    return r.results[0]["out_0_dram"]
```

```python
from contextlib import ExitStack

import concourse.bass as bass
from concourse import mybir

F32 = mybir.dt.float32
BF16 = mybir.dt.bfloat16
I32 = mybir.dt.int32
I16 = mybir.dt.int16
ALU = mybir.AluOpType
ACT = mybir.ActivationFunctionType
AX_X = mybir.AxisListType.X

P = 128
HEADS = 8
PARTS = 3
WIN = P // PARTS
ROWS_W = WIN * PARTS
TILES = 4
ROWS = P * TILES
RING = 4
EPS = 1e-5
Z_EPS = 1e-6
CLIP = 5.0
ROUND = 1.5 * 2.0 ** 23


def graph_attention_then_sage_kernel(nc, x, src, dst, edge_attr, Wq, bq, Wk, bk, We, be, Wv, bv,
                                     Wl, bl, Wr, gamma, beta, out):
    N, D = x.shape
    E = src.shape[0]
    DH = D // HEADS
    KV = 2 * D
    KVQ = 3 * D
    MSG = D + HEADS
    NB = -(-(-(-E // ROWS)) // RING) * RING
    RINGS = NB // RING
    G = -(-N // ROWS)
    NT = G * TILES
    NPAD = G * ROWS
    FULL = N // P
    REST = N - FULL * P
    USED = -(-N // P)
    LASTB = NB - RING
    QCH = NB // 4
    WHOLE = E // ROWS
    assert G % 2 == 1 and NB % 4 == 0 and QCH <= P and WHOLE > 3 * QCH and N + WIN <= NPAD and N < 2 ** 15
    assert USED <= RINGS <= NT

    def start_of(b):
        return min(b * ROWS, E - ROWS) if isinstance(b, int) else b * ROWS

    def repeated_partitions(b):
        return min(max(b * ROWS - (E - ROWS), 0), ROWS) // TILES

    kv_tab = nc.dram_tensor("kv_tab", [NPAD, KV], F32, kind="Internal").ap()
    q_tab = nc.dram_tensor("q_tab", [NPAD * PARTS, D], BF16, kind="Internal").ap()
    rel_tab = nc.dram_tensor("rel_tab", [NB, ROWS], I16, kind="Internal").ap()
    h1_tab = nc.dram_tensor("h1_tab", [NPAD, D], F32, kind="Internal").ap()

    def node_rows(table, g):
        return table[bass.ds(g * ROWS, ROWS), :].rearrange("(t p) f -> p t f", p=P)

    def edges(vec, b):
        return vec[bass.ds(start_of(b), ROWS)]

    with ExitStack() as ctx:
        def sb(name, shape, dt=F32):
            return ctx.enter_context(nc.sbuf_tensor(name, shape, dt))

        def sem(name):
            return ctx.enter_context(nc.semaphore(name))

        x_sb = sb("x_sb", [P, NT, D])
        h_sb = sb("h_sb", [P, NT, D])
        acc = sb("acc", [MSG, NPAD])
        ident = sb("ident", [P, P])
        ones = sb("ones", [P, P])
        eps = sb("eps", [P, 1])
        iota_w = sb("iota_w", [P, WIN])
        wkvq = sb("wkvq", [D + 1, KVQ])
        we = sb("we", [D + 1, D])
        wl_in = sb("wl_in", [D, D])
        wr_in = sb("wr_in", [D, D])
        wl = sb("wl", [D + 1, D + 1])
        wr = sb("wr", [D + 1, D])
        gamma_b = sb("gamma_b", [P, D])
        beta_b = sb("beta_b", [P, D])
        dst_rel0 = sb("dst_rel0", [P, NB, TILES])
        dst_rel = sb("dst_rel", [P, NB, TILES])
        row_node = sb("row_node", [P, 1])
        base_i = sb("base_i", [1, NB], I32)
        passes_i = sb("passes_i", [1, 1], I32)
        h_flat = h_sb[:, :, :].rearrange("p t f -> p (t f)")
        taken = [0]

        def setup_only(columns):
            taken[0] += columns
            return h_flat[:, taken[0] - columns:taken[0]]
        dst_i = setup_only(NB * TILES).bitcast(I32).rearrange("p (b t) -> p b t", t=TILES)
        dst_f = setup_only(NB * TILES).rearrange("p (b t) -> p b t", t=TILES)
        dst_nat = setup_only(4 * ROWS).bitcast(I32).rearrange("q (c e) -> q c e", c=4)
        rel_nat = setup_only(2 * ROWS).bitcast(I16).rearrange("q (c e) -> q c e", c=4)
        diag_mn, diag_mx, base_b, span_b = (setup_only(NB) for _ in range(4))
        col_mn, col_mx = setup_only(4), setup_only(4)
        span_m = setup_only(1)
        third = setup_only(1)
        iota_p = setup_only(1)
        iota_pi = setup_only(1).bitcast(I32)
        iota_i = setup_only(WIN).bitcast(I32)
        kvg = sb("kvg", [P, RING, TILES * KV])
        kv_slot = [kvg[:, k, :].rearrange("p (t f) -> p t f", f=KV) for k in range(RING)]
        h1_slot = [kvg[:, k, 0:TILES * (D + 1)].rearrange("p (t f) -> p t f", f=D + 1) for k in range(RING)]
        idx = sb("idx", [P, RING, TILES], I32)
        ea = sb("ea", [P, RING, TILES, D])
        dst_row = sb("dst_row", [ROWS_W, RING, ROWS], I16)
        q_win = sb("q_win", [ROWS_W, RING, D], BF16)
        ea_t = sb("ea_t", [D + 1, 2, ROWS])
        sel = sb("sel", [P, 2, TILES, WIN])
        sel_t = sb("sel_t", [ROWS_W, 2, TILES, P], BF16)
        prod = sb("prod", [P, TILES * D])
        score = sb("score", [P, TILES * HEADS])
        msg = sb("msg", [P, 2, TILES, MSG])
        node_sum = sb("node_sum", [P, 2, TILES])
        node_sq = sb("node_sq", [P, 2, TILES])
        node_r = sb("node_r", [P, 2, TILES])
        centred = sb("centred", [P, 2, TILES, D])
        squares = msg[:, :, :, 0:D]
        normed = sb("normed", [P, 2, TILES, D])
        h_t = sb("h_t", [D + 1, 2, ROWS])
        kv_out = sb("kv_out", [P, 2, TILES, KV])
        q_out = sb("q_out", [P, 2, TILES, PARTS, D], BF16)
        q_rest = sb("q_rest", [P, 2, TILES, D])
        h_out = q_rest
        rz = sb("rz", [P, 2, TILES * HEADS])
        own_rows = centred[:, 0, 0, :]
        h_sum = prod[:, :]
        mean_b = normed[:, 0, 0, :]
        scale_b = normed[:, 0, 1, :]
        acc_stage = [kv_out[:, k, :, :].rearrange("p t f -> p (t f)")[:, 0:ROWS] for k in range(2)]

        psum = ctx.enter_context(nc.psum_tensor("psum", [P, 8, 512], F32))
        bank = [psum[:, i, :] for i in range(8)]
        b_tr, b_e, b_q, b_agg = bank[0:2], bank[2:4], bank[4:6], bank[6:8]
        node_banks = [psum[:, TILES * k:TILES * (k + 1), :] for k in range(2)]

        s_const = sem("s_const")
        s_x_first = sem("s_x_first")
        s_x = sem("s_x")
        s_dst = sem("s_dst")
        s_dst_nat = sem("s_dst_nat")
        s_idx = [sem(f"s_idx{k}") for k in range(RING)]
        s_ea = [sem(f"s_ea{k}") for k in range(RING)]
        s_dstrow = [sem(f"s_dstrow{k}") for k in range(RING)]
        s_qwin = [sem(f"s_qwin{k}") for k in range(RING)]
        s_kv = [sem(f"s_kv{k}") for k in range(RING)]
        s_idx1 = [sem(f"s_idx1{k}") for k in range(RING)]
        s_h1g = [sem(f"s_h1g{k}") for k in range(RING)]
        s_gate = sem("s_gate")
        s_pool = sem("s_pool")
        s_iota = sem("s_iota")
        s_wq = sem("s_wq")
        s_wt = sem("s_wt")
        s_wt_sb = sem("s_wt_sb")
        s_win_step = sem("s_win_step")
        s_rel = sem("s_rel")
        s_relst = sem("s_relst")
        s_diag = sem("s_diag")
        s_bc = sem("s_bc")
        s_base = sem("s_base")
        s_sum_step = sem("s_sum_step")
        s_rstd_step = sem("s_rstd_step")
        s_cent = sem("s_cent")
        s_sq = sem("s_sq")
        s_sqsum = sem("s_sqsum")
        s_std = sem("s_std")
        s_normed = sem("s_normed")
        s_ht_ps = sem("s_ht_ps")
        s_ht = sem("s_ht")
        s_kvq = sem("s_kvq")
        s_kv_out = sem("s_kv_out")
        s_qrest = sem("s_qrest")
        s_qmid = sem("s_qmid")
        s_qlow = sem("s_qlow")
        s_kvst = [sem(f"s_kvst{k}") for k in range(2)]
        s_qst = [sem(f"s_qst{k}") for k in range(2)]
        s_ea_ps = sem("s_ea_ps")
        s_ea_t = sem("s_ea_t")
        s_e = sem("s_e")
        s_q = sem("s_q")
        s_sel_t = sem("s_sel_t")
        s_kq = sem("s_kq")
        s_kqe = sem("s_kqe")
        s_dot = sem("s_dot")
        s_clip = sem("s_clip")
        s_exp = sem("s_exp")
        s_msg = sem("s_msg")
        s_agg = sem("s_agg")
        s_acc = sem("s_acc")
        s_pass = sem("s_pass")
        s_ones_col = sem("s_ones_col")
        s_mst = sem("s_mst")
        s_mt = sem("s_mt")
        s_z_step = sem("s_z_step")
        s_hout = sem("s_hout")
        s_res = sem("s_res")
        s_msum_step = sem("s_msum_step")
        s_mcent = sem("s_mcent")
        s_msq = sem("s_msq")
        s_msqsum = sem("s_msqsum")
        s_mstd = sem("s_mstd")
        s_mrstd = sem("s_mrstd")
        s_h1 = sem("s_h1")
        s_h1st = [sem(f"s_h1st{k}") for k in range(2)]
        s_acc0 = sem("s_acc0")
        s_sel1 = sem("s_sel1")
        s_agg1 = sem("s_agg1")
        s_acc1 = sem("s_acc1")
        s_pass1 = sem("s_pass1")
        s_own_ld = sem("s_own_ld")
        s_own_ps = sem("s_own_ps")
        s_own_t = sem("s_own_t")
        s_own_lin = sem("s_own_lin")
        s_own_h = sem("s_own_h")
        s_fst = sem("s_fst")
        s_lin = sem("s_lin")
        s_deg_step = sem("s_deg_step")
        s_neigh = sem("s_neigh")
        s_hh = sem("s_hh")
        s_hsum = sem("s_hsum")
        s_sum = sem("s_sum")
        s_bn_step = sem("s_bn_step")
        s_hc = sem("s_hc")
        s_fsq = sem("s_fsq")
        s_var = sem("s_var")
        s_bsq = sem("s_bsq")
        s_bstd = sem("s_bstd")
        s_scaled = sem("s_scaled")
        s_shifted = sem("s_shifted")
        s_o = sem("s_o")
        s_out = sem("s_out")

        CONSTS = 13
        PADDED, IOTAS, IDENTITY, ONE, ONE_ROWS, CLEARED = 1, 3, 5, 7, 11, 12
        X_LOADS = 4

        def passes(eng):
            eng.wait_ge(s_base, 1)
            return eng.value_load(passes_i[0:1, 0:1], min_val=1, max_val=N // WIN + 1)

        def base_of(eng, b, w):
            first = eng.value_load(base_i[0:1, bass.ds(b, 1)], min_val=0, max_val=N - 1)
            node = first + w * WIN
            return (node + (node > N) * (N - node)).with_bounds(min_val=0, max_val=N)

        def edge_steps(eng, w, step):
            def one(b, k, j):
                step(b, k, w * NB + b, w * RINGS + j,
                     isinstance(b, int) and b == 0, isinstance(b, int) and b == NB - 1)
            for k in range(RING):
                one(k, k, 0)
            with eng.Fori(1, RINGS - 1) as j:
                for k in range(RING):
                    one(j * RING + k, k, j)
            for k in range(RING):
                one(LASTB + k, k, RINGS - 1)

        def node_stages(eng, *stages):
            depth = max(behind for behind, fn in stages)
            start = max(2, depth + depth % 2)
            rounds = (G - start) // 2

            def apart(s):
                for behind, fn in stages:
                    if 0 <= s - behind < G:
                        fn(s - behind, (s - behind) % 2, (s - behind) // 2)
            for s in range(start):
                apart(s)
            with eng.Fori(0, rounds) as r:
                for s in (start, start + 1):
                    for behind, fn in stages:
                        fn(r * 2 + (s - behind), (s - behind) % 2, r + (s - behind) // 2)
            for s in range(start + 2 * rounds, G + depth):
                apart(s)

        def stores(k):
            return 16 * ((G + 1 - k) // 2 + 1)

        def used_rows(g, t):
            return min(max(N - g * ROWS - t * P, 0), P)

        def is_last(g):
            return isinstance(g, int) and g == G - 1

        def group(g):
            return bass.ds(g * TILES, TILES)

        block = ctx.enter_context(nc.Block())

        @block.sync
        def _(sp):
            for s, count in ((s_ea_t, 2), (s_e, 2), (s_q, 2), (s_kq, 2), (s_kqe, 2), (s_msg, RING),
                             (s_agg, 2), (s_acc, 2), (s_agg1, RING), (s_acc1, 2), (s_sel1, 2),
                             (s_ht_ps, 2), (s_ht, 2), (s_kvq, 2), (s_kv_out, 2), (s_qrest, 2), (s_qlow, 2),
                             (s_kvst[0], 16), (s_kvst[1], 16), (s_qst[0], 16), (s_qst[1], 16),
                             (s_mt, 2), (s_hout, 2), (s_res, 2), (s_h1, 2), (s_h1st[0], 16), (s_h1st[1], 16),
                             (s_own_ps, 1), (s_own_t, 1), (s_own_lin, 1), (s_own_h, 1),
                             (s_lin, 2), (s_neigh, 2), (s_fsq, 2), (s_var, 2)):
                sp.sem_inc(s, count)
            sp.dma_start(dst_nat[0:QCH, 0:3, :],
                         dst[0:3 * QCH * ROWS].rearrange("(c q e) -> q c e", c=3, e=ROWS)).then_inc(s_dst_nat, 16)
            sp.dma_start(dst_nat[0:WHOLE - 3 * QCH, 3, :],
                         dst[3 * QCH * ROWS:WHOLE * ROWS].rearrange("(q e) -> q e", e=ROWS)).then_inc(s_dst_nat, 16)
            for b in range(WHOLE, NB):
                sp.dma_start(dst_nat[b - 3 * QCH:b - 3 * QCH + 1, 3, :],
                             edges(dst, b).rearrange("(a e) -> a e", a=1)).then_inc(s_dst_nat, 16)
            sp.dma_start(dst_i[:, 0:WHOLE, :],
                         dst[0:WHOLE * ROWS].rearrange("(b p t) -> p b t", p=P, t=TILES)).then_inc(s_dst, 16)
            for b in range(WHOLE, NB):
                sp.dma_start(dst_i[:, b, :], edges(dst, b).rearrange("(p t) -> p t", t=TILES)).then_inc(s_dst, 16)
            tile_rows = lambda t0, t1: x[t0 * P:t1 * P, :].rearrange("(t p) f -> p t f", p=P)
            sp.dma_start(x_sb[:, 0:TILES, :], tile_rows(0, TILES)).then_inc(s_x_first, 16)
            row = lambda v: v.rearrange("(a d) -> a d", a=1)
            for to, of in ((wkvq[0:D, KV:KVQ], Wq), (wkvq[D:D + 1, KV:KVQ], row(bq)),
                           (wkvq[0:D, 0:D], Wk), (wkvq[0:D, D:KV], Wv), (wkvq[D:D + 1, 0:D], row(bk)),
                           (wkvq[D:D + 1, D:KV], row(bv)), (wl_in[:, :], Wl), (wr_in[:, :], Wr),
                           (we[0:D, :], We), (we[D:D + 1, :], row(be)),
                           (wr[D:D + 1, :], row(bl)), (gamma_b[:, :], row(gamma).to_broadcast([P, D])),
                           (beta_b[:, :], row(beta).to_broadcast([P, D]))):
                sp.dma_start(to, of).then_inc(s_const, 16)
            chunk = -(-(FULL - TILES) // X_LOADS)
            for t0 in range(TILES, FULL, chunk):
                t1 = min(t0 + chunk, FULL)
                sp.dma_start(x_sb[:, t0:t1, :], tile_rows(t0, t1)).then_inc(s_x, 16)
            sp.wait_ge(s_pool, PADDED)
            sp.dma_start(x_sb[0:REST, FULL, :], x[FULL * P:N, :]).then_inc(s_x, 16)
            sp.wait_ge(s_rel, 4)
            sp.dma_start(rel_tab.rearrange("(c q) e -> q c e", c=4), rel_nat[0:QCH, :, :]).then_inc(s_relst, 16)

            def store_tables(g, k, j):
                sp.wait_ge(s_kv_out, g + 3)
                sp.dma_start(node_rows(kv_tab, g), kv_out[:, k, :, :]).then_inc(s_kvst[k], 16)
                sp.wait_ge(s_qlow, g + 3)
                sp.dma_start(q_tab[bass.ds(g * ROWS * PARTS, ROWS * PARTS), :]
                             .rearrange("(t p s) f -> p t (s f)", p=P, s=PARTS),
                             q_out[:, k, :, :, :].rearrange("p t s f -> p t (s f)")).then_inc(s_qst[k], 16)
            node_stages(sp, (0, store_tables))
            sp.wait_ge(s_relst, 16)
            for k in range(2):
                sp.wait_ge(s_qst[k], stores(k))

            with sp.Fori(0, passes(sp)) as w:
                def load(b, k, n, turn, first, last):
                    sp.wait_ge(s_msg, n + 1)
                    sp.dma_start(idx[:, k, :], edges(src, b).rearrange("(p t) -> p t", t=TILES)).then_inc(s_idx[k], 16)
                    sp.dma_start(ea[:, k, :, :], edge_attr[bass.ds(start_of(b), ROWS), :]
                                 .rearrange("(p t) f -> p t f", t=TILES)).then_inc(s_ea[k], 16)
                    sp.dma_start(dst_row[:, k, :], rel_tab[bass.ds(b, 1), :]
                                 .to_broadcast([ROWS_W, ROWS])).then_inc(s_dstrow[k], 16)
                    sp.dma_start(q_win[:, k, :],
                                 q_tab[bass.ds(base_of(sp, b, w) * PARTS, ROWS_W), :]).then_inc(s_qwin[k], 16)
                edge_steps(sp, w, load)

            def store_h1(g, k, j):
                sp.wait_ge(s_h1, g + 3)
                sp.dma_start(node_rows(h1_tab, g), normed[:, k, :, :]).then_inc(s_h1st[k], 16)
            node_stages(sp, (0, store_h1))
            for k in range(2):
                sp.wait_ge(s_h1st[k], stores(k))

            with sp.Fori(0, passes(sp)) as w:
                def load1(b, k, n, turn, first, last):
                    sp.wait_ge(s_agg1, n + 1)
                    sp.dma_start(idx[:, k, :], edges(src, b).rearrange("(p t) -> p t", t=TILES)).then_inc(s_idx1[k], 16)
                    if k == 0:
                        sp.wait_ge(s_own_ps, turn + 1)
                        sp.dma_start(own_rows, h1_tab[bass.ds(b * (P // RING), P), :]).then_inc(s_own_ld, 16)
                edge_steps(sp, w, load1)

            def store_out(g, k, j):
                sp.wait_ge(s_o, g + 1)
                if is_last(g):
                    for t in range(TILES):
                        rows = used_rows(g, t)
                        if rows:
                            at = g * ROWS + t * P
                            sp.dma_start(out[at:at + rows, :], h_sb[0:rows, g * TILES + t, :]).then_inc(s_out, 16)
                else:
                    sp.dma_start(node_rows(out, g), h_sb[:, group(g), :]).then_inc(s_out, 16)
            node_stages(sp, (0, store_out))
            sp.wait_ge(s_out, 16 * (G - 1 + USED - (G - 1) * TILES))

        @block.gpsimd
        def _(pool):
            def made(ins, count=[0]):
                ins.then_inc(s_pool, 1)
                count[0] += 1
                pool.wait_ge(s_pool, count[0])

            made(pool.memset(x_sb[:, FULL:NT, :], 0.0))
            made(pool.iota(iota_i[:, :], pattern=[[1, WIN]], base=0, channel_multiplier=0))
            made(pool.iota(iota_pi[:, :], pattern=[[0, 1]], base=0, channel_multiplier=1))
            made(pool.memset(ident[:, :], 0.0))
            made(pool.affine_select(out=ident[:, :], in_=ident[:, :], compare_op=ALU.not_equal, fill=1.0, base=0,
                                    pattern=[[-1, P]], channel_multiplier=1))
            made(pool.memset(ones[:, :], 1.0))
            made(pool.memset(eps[:, :], EPS))
            made(pool.memset(wl[:, :], 0.0))
            made(pool.memset(wl[D:D + 1, D:D + 1], 1.0))
            made(pool.memset(h_t[D:D + 1, :, :], 1.0))
            made(pool.memset(ea_t[D:D + 1, :, :], 1.0))
            made(pool.memset(acc[:, :], 0.0))

            def split_q(g, k, j):
                pool.wait_ge(s_qrest, g + 3)
                pool.sem_inc(s_gate, 1)
                pool.tensor_copy(q_out[:, k, :, 1, :], q_rest[:, k, :, :]).then_inc(s_qmid, 1)
                pool.wait_ge(s_qmid, g + 1)
                pool.sem_inc(s_gate, 1)
                pool.tensor_tensor(q_out[:, k, :, 2, :], q_rest[:, k, :, :], q_out[:, k, :, 1, :],
                                   ALU.subtract).then_inc(s_qlow, 1)
            node_stages(pool, (0, split_q))

            for k in range(2):
                pool.wait_ge(s_kvst[k], stores(k))
            with pool.Fori(0, passes(pool)) as w:
                def gather(b, k, n, turn, first, last):
                    pool.wait_ge(s_idx[k], (turn + 1) * 16)
                    pool.sem_inc(s_gate, 1)
                    for t in range(TILES):
                        pool.indirect_dma_start(
                            out=kv_slot[k][:, t, :], out_offset=None, in_=kv_tab[:, :],
                            in_offset=bass.IndirectOffsetOnAxis(ap=idx[:, k, t:t + 1], axis=0)).then_inc(s_kv[k], 16)
                edge_steps(pool, w, gather)

            pool.wait_ge(s_acc0, 1)

            def stage(g, k, j):
                pool.wait_ge(s_mt, g + 1)
                pool.sem_inc(s_gate, 1)
                pool.tensor_copy(acc_stage[k][0:MSG, :], acc[:, bass.ds(g * ROWS, ROWS)]).then_inc(s_mst, 1)

            def residual(g, k, j):
                rows = x_sb[:, group(g), :]
                pool.wait_ge(s_hout, g + 3)
                pool.sem_inc(s_gate, 1)
                pool.tensor_tensor(rows, rows, h_out[:, k, :, :], ALU.add).then_inc(s_res, 1)
            node_stages(pool, (0, stage), (1, residual))
            pool.wait_ge(s_mst, G)
            made(pool.memset(acc[0:D + 1, :], 0.0))
            for k in range(RING):
                pool.memset(h1_slot[k][:, :, D:D + 1], 1.0).then_inc(s_ones_col, 1)
                pool.wait_ge(s_ones_col, k + 1)
            if USED < NT:
                made(pool.memset(h_sb[:, USED:NT, :], 0.0))

            for k in range(2):
                pool.wait_ge(s_h1st[k], stores(k))
            with pool.Fori(0, passes(pool)) as w:
                def gather1(b, k, n, turn, first, last):
                    pool.wait_ge(s_idx1[k], (turn + 1) * 16)
                    pool.sem_inc(s_gate, 1)
                    for t in range(TILES):
                        pool.indirect_dma_start(
                            out=h1_slot[k][:, t, 0:D], out_offset=None, in_=h1_tab[:, :],
                            in_offset=bass.IndirectOffsetOnAxis(ap=idx[:, k, t:t + 1], axis=0)).then_inc(s_h1g[k], 16)
                edge_steps(pool, w, gather1)

            def sum_rows(g, k, j):
                pool.wait_ge(s_hh, g + 1)
                if isinstance(g, int) and g == 0:
                    pool.tensor_copy(h_sum.rearrange("p (t f) -> p t f", f=D), h_sb[:, group(g), :]).then_inc(s_hsum, 1)
                    return
                pool.wait_ge(s_hsum, g)
                pool.sem_inc(s_gate, 1)
                if is_last(g):
                    for t in range(TILES):
                        rows = used_rows(g, t)
                        if rows:
                            at = h_sum[0:rows, t * D:(t + 1) * D]
                            pool.tensor_tensor(at, at, h_sb[0:rows, g * TILES + t, :], ALU.add).then_inc(s_hsum, 1)
                else:
                    at = h_sum.rearrange("p (t f) -> p t f", f=D)
                    pool.tensor_tensor(at, at, h_sb[:, group(g), :], ALU.add).then_inc(s_hsum, 1)
            node_stages(pool, (0, sum_rows))

            def shift(g, k, j):
                rows = h_sb[:, group(g), :]
                pool.wait_ge(s_scaled, g + 1)
                pool.sem_inc(s_gate, 1)
                pool.tensor_tensor(rows, rows, beta_b[:, :].unsqueeze(1).to_broadcast([P, TILES, D]),
                                   ALU.add).then_inc(s_shifted, 1)
            node_stages(pool, (0, shift))

        @block.tensor
        def _(pe):
            pe.wait_ge(s_pool, IDENTITY)
            pe.wait_ge(s_const, 16 * CONSTS)
            pe.transpose(bank[6][0:D, 0:D], wl_in[:, :], ident[0:D, 0:D])
            pe.transpose(bank[6][0:D, P:P + D], wr_in[:, :], ident[0:D, 0:D]).then_inc(s_wt, 1)
            pe.wait_ge(s_pool, ONE_ROWS)

            pe.wait_ge(s_diag, 8)
            for c in range(4):
                part = slice(c * QCH, (c + 1) * QCH)
                pe.matmul(bank[2][:, part], ones[0:QCH, :], diag_mn[0:QCH, part], start=True, stop=True)
                mm = pe.matmul(bank[3][:, part], ones[0:QCH, :], diag_mx[0:QCH, part], start=True, stop=True)
            mm.then_inc(s_bc, 1)

            def turn_normed(g, k, j):
                pe.wait_ge(s_normed, g + 1)
                pe.wait_ge(s_kv_out, g + 1)
                pe.wait_ge(s_qrest, g + 1)
                for t in range(TILES):
                    mm = pe.transpose(node_banks[k][0:D, t, KVQ:KVQ + P], normed[:, k, t, :], ident[:, :])
                mm.then_inc(s_ht_ps, 1)

            def project(g, k, j):
                pe.wait_ge(s_ht, g + 3)
                for t in range(TILES):
                    mm = pe.matmul(node_banks[k][:, t, 0:KVQ], h_t[:, k, t * P:(t + 1) * P], wkvq[:, :],
                                   start=True, stop=True)
                mm.then_inc(s_kvq, 1)
            pe.wait_ge(s_wt_sb, 1)
            pe.wait_ge(s_wq, 1)
            pe.wait_ge(s_base, 1)
            node_stages(pe, (0, turn_normed), (1, project))

            pe.wait_ge(s_kv_out, G + 2)
            pe.wait_ge(s_qrest, G + 2)
            with pe.Fori(0, passes(pe)) as w:
                def turn_ea(k, n, turn):
                    pe.wait_ge(s_ea[k], (turn + 1) * 16)
                    pe.wait_ge(s_ea_t, n + 1)
                    for t in range(TILES):
                        mm = pe.transpose(b_tr[k % 2][0:D, t * P:(t + 1) * P], ea[:, k, t, :], ident[:, :])
                    mm.then_inc(s_ea_ps, 1)

                def aggregate(k, n):
                    pe.wait_ge(s_msg, n + 1 + RING)
                    pe.wait_ge(s_acc, n + 1)
                    for t in range(TILES):
                        mm = pe.matmul(b_agg[k % 2][0:MSG, 0:WIN], msg[:, k % 2, t, :], sel[:, k % 2, t, :],
                                       start=(t == 0), stop=(t == TILES - 1))
                    mm.then_inc(s_agg, 1)

                def step(b, k, n, turn, first, last):
                    if first:
                        turn_ea(k, n, turn)
                    if not last:
                        turn_ea((k + 1) % RING, n + 1, turn + (k + 1) // RING)
                    pe.wait_ge(s_ea_t, n + 3)
                    pe.wait_ge(s_kqe, n + 1)
                    for t in range(TILES):
                        mm = pe.matmul(b_e[k % 2][:, t * D:(t + 1) * D], ea_t[:, k % 2, t * P:(t + 1) * P], we[:, :],
                                       start=True, stop=True)
                    mm.then_inc(s_e, 1)
                    pe.wait_ge(s_qwin[k], (turn + 1) * 16)
                    pe.wait_ge(s_sel_t, n + 1)
                    pe.wait_ge(s_kq, n + 1)
                    for t in range(TILES):
                        mm = pe.matmul(b_q[k % 2][:, t * D:(t + 1) * D], sel_t[:, k % 2, t, :], q_win[:, k, :],
                                       start=True, stop=True)
                    mm.then_inc(s_q, 1)
                    if not first:
                        aggregate((k - 1) % RING, n - 1)
                    if last:
                        aggregate(k, n)
                edge_steps(pe, w, step)

            def turn_sums(g, k, j):
                pe.wait_ge(s_mst, g + 1)
                pe.wait_ge(s_hout, g + 1)
                for t in range(TILES):
                    mm = pe.transpose(bank[k][:, t * MSG:(t + 1) * MSG], acc_stage[k][0:MSG, t * P:(t + 1) * P],
                                      ident[0:MSG, 0:MSG])
                mm.then_inc(s_mt, 1)
            node_stages(pe, (0, turn_sums))

            pe.wait_ge(s_ones_col, RING)
            pe.wait_ge(s_hout, G + 2)
            with pe.Fori(0, passes(pe)) as w:
                def step1(b, k, n, turn, first, last):
                    if k == 0:
                        pe.wait_ge(s_own_ld, (turn + 1) * 16)
                        pe.wait_ge(s_own_t, turn + 1)
                        pe.transpose(b_tr[0][0:D, 0:P], own_rows, ident[:, :]).then_inc(s_own_ps, 1)
                    if k == 2:
                        pe.wait_ge(s_own_t, turn + 2)
                        pe.wait_ge(s_own_h, turn + 1)
                        pe.matmul(b_e[0][:, 0:D], h_t[:, 0, 0:P], wr[:, :], start=True, stop=True).then_inc(s_own_lin, 1)
                    pe.wait_ge(s_h1g[k], (turn + 1) * 16 * TILES)
                    pe.wait_ge(s_sel1, n + 3)
                    pe.wait_ge(s_acc1, n + 1)
                    for t in range(TILES):
                        mm = pe.matmul(b_agg[k % 2][0:D + 1, 0:WIN], h1_slot[k][:, t, :], sel[:, k % 2, t, :],
                                       start=(t == 0), stop=(t == TILES - 1))
                    mm.then_inc(s_agg1, 1)
                edge_steps(pe, w, step1)

            def products(g, k, j):
                pe.wait_ge(s_fst, g + 1)
                pe.wait_ge(s_neigh, g + 1)
                for t in range(TILES):
                    mm = pe.matmul(b_q[k][:, t * (D + 1):(t + 1) * (D + 1)], acc_stage[k][0:D + 1, t * P:(t + 1) * P],
                                   wl[:, :], start=True, stop=True)
                mm.then_inc(s_lin, 1)
            node_stages(pe, (0, products))

            pe.wait_ge(s_hsum, G - 1 + USED - (G - 1) * TILES)
            pe.matmul(bank[6][:, 0:TILES * D], ones[:, :], h_sum, start=True, stop=True).then_inc(s_sum, 1)

            def sum_sq(g, k, j):
                pe.wait_ge(s_fsq, g + 3)
                if is_last(g):
                    for t in range(TILES):
                        rows = used_rows(g, t)
                        if rows:
                            mm = pe.matmul(bank[7][:, t * D:(t + 1) * D], ones[0:rows, :], squares[0:rows, k, t, :],
                                           start=False, stop=True, skip_group_check=True)
                else:
                    mm = pe.matmul(bank[7][:, 0:TILES * D], ones[:, :], squares[:, k, :, :],
                                   start=isinstance(g, int) and g == 0, stop=False, skip_group_check=True)
                mm.then_inc(s_var, 1)
            node_stages(pe, (0, sum_sq))

        @block.scalar
        def _(act):
            def deviation(k):
                return nc.scalar.activation(node_sq[:, k, :], node_sq[:, k, :], ACT.Sqrt, bias=eps[:, 0:1], scale=1.0 / D)

            act.wait_ge(s_const, 16 * CONSTS)
            nc.scalar.mul(wkvq[:, KV:KVQ], wkvq[:, KV:KVQ], float(DH) ** -0.5).then_inc(s_wq, 1)
            act.wait_ge(s_pool, ONE)

            def root(g, k, j):
                act.wait_ge(s_sqsum, g + 1)
                deviation(k).then_inc(s_std, 1)

            def parts_out(g, k, j):
                act.wait_ge(s_kvq, g + 3)
                act.wait_ge(s_qst[k], (j + 1) * 16)
                act.wait_ge(s_kvst[k], (j + 1) * 16)
                nc.scalar.copy(q_out[:, k, :, 0, :], node_banks[k][:, :, KV:KVQ])
                nc.scalar.copy(kv_out[:, k, :, :], node_banks[k][:, :, 0:KV]).then_inc(s_kv_out, 1)

            def square(g, k, j):
                act.wait_ge(s_cent, g + 1)
                nc.scalar.activation(squares[:, k, :, :], centred[:, k, :, :], ACT.Square).then_inc(s_sq, 1)

            def cut_off(g, k, j):
                act.wait_ge(s_ht_ps, g + 3)
                act.wait_ge(s_kvq, g + 1)
                nc.scalar.activation(h_t[0:D, k, :].rearrange("f (t p) -> f t p", p=P),
                                     node_banks[k][0:D, :, KVQ:KVQ + P], ACT.Relu).then_inc(s_ht, 1)
            node_stages(act, (1, root), (3, parts_out), (0, square), (1, cut_off))

            with act.Fori(0, passes(act)) as w:
                def copy_ea(k, n):
                    act.wait_ge(s_ea_ps, n + 1)
                    act.wait_ge(s_e, n + 1)
                    nc.scalar.copy(ea_t[0:D, k % 2, :], b_tr[k % 2][0:D, :]).then_inc(s_ea_t, 1)

                def step(b, k, n, turn, first, last):
                    if first:
                        copy_ea(k, n)
                    if not last:
                        copy_ea((k + 1) % RING, n + 1)
                    act.wait_ge(s_clip, n + 1)
                    act.wait_ge(s_agg, n + 1)
                    nc.scalar.activation(msg[:, k % 2, :, D:MSG], score[:, :].rearrange("p (t h) -> p t h", h=HEADS),
                                         ACT.Exp).then_inc(s_exp, 1)
                edge_steps(act, w, step)

            def root1(g, k, j):
                act.wait_ge(s_msqsum, g + 1)
                deviation(k).then_inc(s_mstd, 1)

            def square1(g, k, j):
                act.wait_ge(s_mcent, g + 1)
                nc.scalar.activation(squares[:, k, :, :], centred[:, k, :, :], ACT.Square).then_inc(s_msq, 1)

            def scale_cut(g, k, j):
                act.wait_ge(s_mrstd, g + 1)
                act.wait_ge(s_h1st[k], (j + 1) * 16)
                for t in range(TILES):
                    made = nc.scalar.activation(normed[:, k, t, :], centred[:, k, t, :], ACT.Relu, scale=node_r[:, k, t:t + 1])
                made.then_inc(s_h1, 1)
            node_stages(act, (2, root1), (1, square1), (2, scale_cut))

            with act.Fori(0, passes(act)) as w:
                with act.Fori(0, RINGS) as j:
                    turn = w * RINGS + j
                    act.wait_ge(s_own_ps, turn + 2)
                    act.wait_ge(s_own_lin, turn + 1)
                    nc.scalar.copy(h_t[0:D, 0, 0:P], b_tr[0][0:D, 0:P]).then_inc(s_own_t, 1)
                    act.wait_ge(s_own_lin, turn + 2)
                    act.sem_inc(s_gate, 1)
                    nc.scalar.copy(h_sb[:, bass.ds(j, 1), :].rearrange("p a f -> p (a f)"), b_e[0][:, 0:D]).then_inc(s_own_h, 1)

            act.wait_ge(s_acc0, 2)

            def stage(g, k, j):
                act.wait_ge(s_lin, g + 1)
                act.sem_inc(s_gate, 1)
                nc.scalar.copy(acc_stage[k][0:D + 1, :], acc[0:D + 1, bass.ds(g * ROWS, ROWS)]).then_inc(s_fst, 1)
            node_stages(act, (0, stage))

            def square2(g, k, j):
                act.wait_ge(s_var, g + 1)
                act.wait_ge(s_hc, g + 1)
                act.sem_inc(s_gate, 1)
                nc.scalar.activation(squares[:, k, :, :], h_sb[:, group(g), :], ACT.Square).then_inc(s_fsq, 1)
            node_stages(act, (0, square2))
            act.wait_ge(s_bsq, 1)
            nc.scalar.activation(scale_b, scale_b, ACT.Sqrt, bias=eps[:, 0:1], scale=1.0 / N).then_inc(s_bstd, 1)

        @block.vector
        def _(dve):
            def per_node(v):
                return v.unsqueeze(2).to_broadcast([P, TILES, D])

            def per_feature(v):
                return v.unsqueeze(1).to_broadcast([P, TILES, D])

            def counted(s_step, before):
                count = [0]

                def step(ins):
                    count[0] += 1
                    ins.then_inc(s_step, 1)
                    dve.wait_ge(s_step, before + count[0])
                return step

            def spread(rows, k, own_step, done):
                own_step(nc.vector.reduce_sum(node_sum[:, k, :], rows, AX_X))
                dve.sem_inc(s_gate, 1)
                nc.vector.scalar_tensor_tensor(out=centred[:, k, :, :], in0=per_node(node_sum[:, k, :]), scalar=-1.0 / D,
                                               in1=rows, op0=ALU.mult, op1=ALU.add).then_inc(done, 1)

            step = counted(s_win_step, 0)
            dve.wait_ge(s_dst_nat, 16 * (2 + NB - WHOLE))
            step(nc.vector.tensor_reduce(col_mn[0:QCH, :], dst_nat[0:QCH, :, :], AX_X, ALU.min))
            step(nc.vector.tensor_reduce(col_mx[0:QCH, :], dst_nat[0:QCH, :, :], AX_X, ALU.max))
            dve.wait_ge(s_pool, IDENTITY)
            for c in range(4):
                for diag, col in ((diag_mn, col_mn), (diag_mx, col_mx)):
                    nc.vector.tensor_scalar(diag[0:QCH, c * QCH:(c + 1) * QCH], ident[0:QCH, 0:QCH], col[0:QCH, c:c + 1],
                                            None, ALU.mult).then_inc(s_diag, 1)
            for c in range(4):
                nc.vector.tensor_scalar(rel_nat[0:QCH, c, :], dst_nat[0:QCH, c, :], col_mn[0:QCH, c:c + 1],
                                        None, ALU.subtract).then_inc(s_rel, 1)
            dve.wait_ge(s_dst, 16 * (1 + NB - WHOLE))
            step(nc.vector.tensor_copy(dst_f, dst_i))
            step(nc.vector.tensor_copy(iota_p, iota_pi))
            step(nc.vector.tensor_scalar(third, iota_p, (PARTS - 1) / 2.0, 1.0 / PARTS, ALU.subtract, ALU.mult))
            step(nc.vector.tensor_scalar(third, third, ROUND, None, ALU.add))
            step(nc.vector.tensor_scalar(row_node[:, :], third, ROUND, -float(WIN), ALU.subtract, ALU.add))
            nc.vector.tensor_copy(iota_w[:, :], iota_i[:, :])
            dve.wait_ge(s_bc, 1)
            step(nc.vector.tensor_copy(base_b, bank[2][:, 0:NB]))
            step(nc.vector.tensor_tensor(span_b, bank[3][:, 0:NB], base_b, ALU.subtract))
            step(nc.vector.tensor_reduce(span_m, span_b, AX_X, ALU.max))
            step(nc.vector.tensor_scalar(span_m, span_m, (WIN - 1) / 2.0, 1.0 / WIN, ALU.subtract, ALU.mult))
            step(nc.vector.tensor_scalar(span_m, span_m, ROUND, None, ALU.add))
            step(nc.vector.tensor_scalar(span_m, span_m, ROUND, 1.0, ALU.subtract, ALU.add))
            step(nc.vector.tensor_copy(passes_i[0:1, :], span_m[0:1, :]))
            step(nc.vector.tensor_tensor(dst_rel0[:, :, :], dst_f,
                                         base_b.unsqueeze(2).to_broadcast([P, NB, TILES]), ALU.subtract))
            step(nc.vector.tensor_scalar(dst_rel0[:, :, :], dst_rel0[:, :, :], float(WIN), None, ALU.add))
            for b in range(WHOLE, NB):
                rep = repeated_partitions(b)
                if rep:
                    step(nc.vector.memset(dst_rel0[0:rep, b, :], -1.0))
            step(nc.vector.tensor_copy(dst_rel[:, :, :], dst_rel0[:, :, :]))
            nc.vector.tensor_copy(base_i[0:1, :], base_b[0:1, :]).then_inc(s_base, 1)
            dve.wait_ge(s_wt, 1)
            dve.wait_ge(s_pool, ONE_ROWS)
            nc.vector.tensor_copy(wl[0:D, 0:D], bank[6][0:D, 0:D])
            nc.vector.tensor_copy(wr[0:D, :], bank[6][0:D, P:P + D]).then_inc(s_wt_sb, 1)

            def sum_squares(g, k, j):
                dve.wait_ge(s_sq, g + 1)
                nc.vector.reduce_sum(node_sq[:, k, :], squares[:, k, :, :], AX_X).then_inc(s_sqsum, 1)

            def centre(g, k, j):
                if isinstance(g, int) and g <= 1:
                    dve.wait_ge(*((s_x_first, 16) if g == 0 else (s_x, 16 * (X_LOADS + 1))))
                spread(x_sb[:, group(g), :], k, counted(s_sum_step, g), s_cent)

            def scale(g, k, j):
                dve.wait_ge(s_std, g + 1)
                counted(s_rstd_step, g)(nc.vector.reciprocal(node_r[:, k, :], node_sq[:, k, :]))
                dve.wait_ge(s_ht_ps, g + 1)
                nc.vector.tensor_tensor(normed[:, k, :, :], centred[:, k, :, :], per_node(node_r[:, k, :]),
                                        ALU.mult).then_inc(s_normed, 1)

            def rest_of_q(g, k, j):
                dve.wait_ge(s_kv_out, g + 3)
                dve.wait_ge(s_qlow, g + 1)
                nc.vector.tensor_tensor(q_rest[:, k, :, :], node_banks[k][:, :, KV:KVQ], q_out[:, k, :, 0, :],
                                        ALU.subtract).then_inc(s_qrest, 1)
            node_stages(dve, (1, sum_squares), (0, centre), (1, scale), (3, rest_of_q))

            def move_windows(done, w, turned):
                nc.vector.tensor_scalar(dst_rel[:, :, :], dst_rel[:, :, :], float(WIN), None,
                                        ALU.subtract).then_inc(done, 1)
                if turned:
                    nc.vector.tensor_scalar(row_node[:, :], row_node[:, :], float(WIN), None, ALU.add).then_inc(done, 1)
                dve.wait_ge(done, (w + 1) * (2 if turned else 1))

            def select(b, k):
                return nc.vector.tensor_tensor(
                    sel[:, k % 2, :, :], iota_w[:, :].unsqueeze(1).to_broadcast([P, TILES, WIN]),
                    dst_rel[:, bass.ds(b, 1), :].rearrange("p a t -> p (a t)").unsqueeze(2).to_broadcast([P, TILES, WIN]),
                    ALU.is_equal)

            def add_sums(b, k, w, n, rows, s_from, credit, s_done):
                at = acc[0:rows, bass.ds(base_of(dve, b, w), WIN)]
                dve.wait_ge(s_from, n + 1 + credit)
                dve.wait_ge(s_done, n + 2)
                dve.sem_inc(s_gate, 1)
                nc.vector.tensor_tensor(at, at, b_agg[k % 2][0:rows, 0:WIN], ALU.add).then_inc(s_done, 1)

            dve.wait_ge(s_pool, CLEARED)
            with dve.Fori(0, passes(dve)) as w:
                move_windows(s_pass, w, True)

                def select_t(b, k, n, turn):
                    dve.wait_ge(s_dstrow[k], (turn + 1) * 16)
                    dve.wait_ge(s_q, n + 1)
                    nc.vector.tensor_scalar(sel_t[:, k % 2, :, :], dst_row[:, k, :].rearrange("w (p t) -> w t p", t=TILES),
                                            row_node[0:ROWS_W, 0:1], None, ALU.is_equal).then_inc(s_sel_t, 1)

                def step(b, k, n, turn, first, last):
                    if first:
                        select_t(b, k, n, turn)
                    heads = lambda v: v.rearrange("p t (h d) -> p t h d", h=HEADS)
                    p3 = prod[:, :].rearrange("p (t f) -> p t f", f=D)
                    dve.wait_ge(s_kv[k], (turn + 1) * 16 * TILES)
                    dve.wait_ge(s_q, n + 3)
                    nc.vector.tensor_tensor(p3, kv_slot[k][:, :, 0:D], b_q[k % 2][:, 0:TILES * D]
                                            .rearrange("p (t f) -> p t f", f=D), ALU.mult).then_inc(s_kq, 1)
                    if not last:
                        select_t(b + 1, (k + 1) % RING, n + 1, turn + (k + 1) // RING)
                    dve.wait_ge(s_e, n + 3)
                    dve.wait_ge(s_kq, n + 3)
                    nc.vector.tensor_tensor(prod[:, :], prod[:, :], b_e[k % 2][:, 0:TILES * D], ALU.mult).then_inc(s_kqe, 1)
                    dve.wait_ge(s_agg, n + 1)
                    dve.sem_inc(s_gate, 1)
                    select(b, k)
                    dve.wait_ge(s_kqe, n + 3)
                    nc.vector.reduce_sum(score[:, :], prod[:, :].rearrange("p (g d) -> p g d", d=DH), AX_X).then_inc(s_dot, 1)
                    if not first:
                        add_sums(b - 1, (k - 1) % RING, w, n - 1, MSG, s_agg, 2, s_acc)
                    dve.wait_ge(s_dot, n + 1)
                    nc.vector.tensor_scalar(score[:, :], score[:, :], -CLIP, CLIP, ALU.max, ALU.min).then_inc(s_clip, 1)
                    dve.wait_ge(s_exp, n + 1)
                    nc.vector.tensor_tensor(heads(msg[:, k % 2, :, 0:D]), heads(kv_slot[k][:, :, D:KV]),
                                            msg[:, k % 2, :, D:MSG].unsqueeze(3).to_broadcast([P, TILES, HEADS, DH]),
                                            ALU.mult).then_inc(s_msg, 1)
                    if last:
                        add_sums(b, k, w, n, MSG, s_agg, 2, s_acc)
                edge_steps(dve, w, step)
            turns = passes(dve)
            dve.wait_ge(s_acc, turns * NB + 2)
            nc.vector.tensor_copy(dst_rel[:, :, :], dst_rel0[:, :, :]).then_inc(s_acc0, 1)

            def sum_squares1(g, k, j):
                dve.wait_ge(s_msq, g + 1)
                nc.vector.reduce_sum(node_sq[:, k, :], squares[:, k, :, :], AX_X).then_inc(s_msqsum, 1)

            def weighted_mean(g, k, j):
                own_step = counted(s_z_step, g * 2)
                sums = bank[k][:, 0:TILES * MSG].rearrange("p (t f) -> p t f", f=MSG)
                z = rz[:, k, :].rearrange("p (t h) -> p t h", h=HEADS)
                heads = lambda v: v.rearrange("p t (h d) -> p t h d", h=HEADS)
                dve.wait_ge(s_mt, g + 3)
                own_step(nc.vector.tensor_scalar(z, sums[:, :, D:MSG], Z_EPS, None, ALU.add))
                own_step(nc.vector.reciprocal(z, z))
                dve.wait_ge(s_res, g + 1)
                nc.vector.tensor_tensor(heads(h_out[:, k, :, :]), heads(sums[:, :, 0:D]),
                                        z.unsqueeze(3).to_broadcast([P, TILES, HEADS, DH]), ALU.mult).then_inc(s_hout, 1)

            def centre1(g, k, j):
                dve.wait_ge(s_res, g + 3)
                dve.wait_ge(s_h1, g + 1)
                dve.sem_inc(s_gate, 1)
                spread(x_sb[:, group(g), :], k, counted(s_msum_step, g), s_mcent)

            def factor1(g, k, j):
                dve.wait_ge(s_mstd, g + 1)
                nc.vector.reciprocal(node_r[:, k, :], node_sq[:, k, :]).then_inc(s_mrstd, 1)
            node_stages(dve, (2, sum_squares1), (0, weighted_mean), (1, centre1), (2, factor1))

            dve.wait_ge(s_pool, CLEARED + 1)
            with dve.Fori(0, turns) as w:
                move_windows(s_pass1, w, False)

                def step1(b, k, n, turn, first, last):
                    dve.wait_ge(s_agg1, n + 3)
                    dve.sem_inc(s_gate, 1)
                    select(b, k).then_inc(s_sel1, 1)
                    if not first:
                        add_sums(b - 1, (k - 1) % RING, w, n - 1, D + 1, s_agg1, RING, s_acc1)
                    if last:
                        add_sums(b, k, w, n, D + 1, s_agg1, RING, s_acc1)
                edge_steps(dve, w, step1)
            dve.wait_ge(s_acc1, turns * NB + 2)
            nc.vector.memset(rz[:, :, :], 0.0).then_inc(s_acc0, 1)

            dve.wait_ge(s_own_h, turns * RINGS + 1)
            if USED < NT:
                dve.wait_ge(s_pool, CLEARED + 2)

            def products_of(k):
                return b_q[k][:, 0:TILES * (D + 1)].rearrange("p (t f) -> p t f", f=D + 1)

            def degree(g, k, j):
                own_step = counted(s_deg_step, g * 2)
                dve.wait_ge(s_lin, g + 3)
                dve.sem_inc(s_gate, 1)
                own_step(nc.vector.tensor_scalar(node_sum[:, k, :].unsqueeze(2), products_of(k)[:, :, D:D + 1], 1.0, None, ALU.max))
                own_step(nc.vector.reciprocal(node_r[:, k, :], node_sum[:, k, :]))

            def neighbours(g, k, j):
                nc.vector.tensor_tensor(centred[:, k, :, :], products_of(k)[:, :, 0:D], per_node(node_r[:, k, :]),
                                        ALU.mult).then_inc(s_neigh, 1)

            def add_own(g, k, j):
                rows = h_sb[:, group(g), :]
                dve.wait_ge(s_neigh, g + 3)
                dve.sem_inc(s_gate, 1)
                nc.vector.tensor_tensor(rows, rows, centred[:, k, :, :], ALU.add).then_inc(s_hh, 1)
            node_stages(dve, (0, degree), (1, add_own), (0, neighbours))

            def over_tiles(sums):
                return sums[:, 0:TILES * D].rearrange("p (t f) -> p f t", f=D)
            step = counted(s_bn_step, 0)
            dve.wait_ge(s_sum, 1)
            step(nc.vector.reduce_sum(mean_b, over_tiles(bank[6]), AX_X))
            step(nc.vector.tensor_scalar(mean_b, mean_b, 1.0 / N, None, ALU.mult))

            def centre_h(g, k, j):
                rows = h_sb[:, group(g), :]
                nc.vector.tensor_tensor(rows, rows, per_feature(mean_b), ALU.subtract).then_inc(s_hc, 1)
            node_stages(dve, (0, centre_h))
            dve.wait_ge(s_const, 16 * CONSTS)
            dve.wait_ge(s_var, G + 2)
            nc.vector.reduce_sum(scale_b, over_tiles(bank[7]), AX_X).then_inc(s_bsq, 1)
            dve.wait_ge(s_bstd, 1)
            step(nc.vector.reciprocal(scale_b, scale_b))
            step(nc.vector.tensor_tensor(scale_b, scale_b, gamma_b[:, :], ALU.mult))

            def scale_h(g, k, j):
                rows = h_sb[:, group(g), :]
                dve.wait_ge(s_fsq, g + 3)
                dve.sem_inc(s_gate, 1)
                nc.vector.tensor_tensor(rows, rows, per_feature(scale_b), ALU.mult).then_inc(s_scaled, 1)

            def finish(g, k, j):
                rows = h_sb[:, group(g), :]
                dve.wait_ge(s_shifted, g + 1)
                dve.sem_inc(s_gate, 1)
                nc.vector.scalar_tensor_tensor(out=rows, in0=rows, scalar=0.0, in1=x_sb[:, group(g), :],
                                               op0=ALU.max, op1=ALU.add).then_inc(s_o, 1)
            node_stages(dve, (0, scale_h), (2, finish))


_INS = ['x', 'src', 'dst', 'edge_attr_96', 'L0_gnn_Wq', 'L0_gnn_bq', 'L0_gnn_Wk', 'L0_gnn_bk', 'L0_gnn_We', 'L0_gnn_be',
        'L0_gnn_Wv', 'L0_gnn_bv', 'L1_gnn_Wl', 'L1_gnn_bl', 'L1_gnn_Wr', 'L1_gnn_gamma', 'L1_gnn_beta']


def kernel(**inputs):
    import numpy as _np
    import concourse.bacc as _bacc
    from concourse import mybir as _mybir
    from concourse.bass_utils import run_bass_kernel_spmd as _run

    nc = _bacc.Bacc("TRN2", target_bir_lowering=False, num_devices=1)
    arrays, args = {}, []
    for name in _INS:
        a = _np.ascontiguousarray(inputs[name])
        arrays[f"in_{name}_dram"] = a
        args.append(nc.dram_tensor(f"in_{name}_dram", a.shape, _mybir.dt.from_np(a.dtype), kind="ExternalInput").ap())
    out = nc.dram_tensor("out_0_dram", arrays["in_x_dram"].shape, _mybir.dt.float32, kind="ExternalOutput").ap()
    graph_attention_then_sage_kernel(nc, *args, out)
    r = _run(nc, [arrays], core_ids=[0])
    return r.results[0]["out_0_dram"]
```

```python
from contextlib import ExitStack

import concourse.bass as bass
from concourse import mybir

F32 = mybir.dt.float32
BF16 = mybir.dt.bfloat16
I32 = mybir.dt.int32
I16 = mybir.dt.int16
ALU = mybir.AluOpType
ACT = mybir.ActivationFunctionType
AX_X = mybir.AxisListType.X

P = 128
HEADS = 8
PARTS = 3
WIN = P // PARTS
ROWS_W = WIN * PARTS
TILES = 4
ROWS = P * TILES
RING = 4
EPS = 1e-5
Z_EPS = 1e-6
CLIP = 5.0
ROUND = 1.5 * 2.0 ** 23


def graph_attention_then_sage_kernel(nc, x, src, dst, edge_attr_t, Wq, bq, Wk, bk, We, be, Wv, bv,
                                     Wl, bl, Wr, gamma, beta, out):
    N, D = x.shape
    E = src.shape[0]
    DH = D // HEADS
    KV = 2 * D
    KVQ = 3 * D
    MSG = D + HEADS
    NB = -(-(-(-E // ROWS)) // RING) * RING
    RINGS = NB // RING
    G = -(-N // ROWS)
    NT = G * TILES
    NPAD = G * ROWS
    FULL = N // P
    REST = N - FULL * P
    USED = -(-N // P)
    LASTB = NB - RING
    STRIDE = (RINGS - 2) // (G - 1)
    BPG = STRIDE * RING
    LATE = RING - 1
    QCH = NB // 4
    WHOLE = E // ROWS
    assert G % 2 == 1 and NB % 4 == 0 and QCH <= P and WHOLE > 3 * QCH and N + WIN <= NPAD and N < 2 ** 15
    assert RINGS - 2 == STRIDE * (G - 1)

    def start_of(b):
        return min(b * ROWS, E - ROWS) if isinstance(b, int) else b * ROWS

    def only_repeats(b):
        return isinstance(b, int) and repeated_partitions(b) == P

    def gathers(k, w, j):
        return w * sum(not only_repeats(b) for b in range(k, NB, RING)) + (j + 1)

    def repeated_partitions(b):
        return min(max(b * ROWS - (E - ROWS), 0), ROWS) // TILES

    kv_tab = nc.dram_tensor("kv_tab", [NPAD, KV], F32, kind="Internal").ap()
    q_tab = nc.dram_tensor("q_tab", [NPAD * PARTS, D], BF16, kind="Internal").ap()
    rel_tab = nc.dram_tensor("rel_tab", [NB, ROWS], I16, kind="Internal").ap()
    h1_tab = nc.dram_tensor("h1_tab", [NPAD, D], F32, kind="Internal").ap()

    def node_rows(table, g):
        return table[bass.ds(g * ROWS, ROWS), :].rearrange("(t p) f -> p t f", p=P)

    def edges(vec, b):
        return vec[bass.ds(start_of(b), ROWS)]

    with ExitStack() as ctx:
        def sb(name, shape, dt=F32):
            return ctx.enter_context(nc.sbuf_tensor(name, shape, dt))

        def sem(name):
            return ctx.enter_context(nc.semaphore(name))

        x_sb = sb("x_sb", [P, NT, D])
        h_sb = sb("h_sb", [P, NT, D])
        acc = sb("acc", [MSG, NPAD])
        ident = sb("ident", [P, P])
        ones = sb("ones", [P, P])
        eps = sb("eps", [P, 1])
        zero = sb("zero", [P, 1])
        iota_w = sb("iota_w", [P, WIN])
        wkvq = sb("wkvq", [D + 1, KVQ])
        we = sb("we", [D + 1, D])
        wl_in = sb("wl_in", [D, D])
        wr_in = sb("wr_in", [D, D])
        wl = sb("wl", [D + 1, D + 1])
        wr = sb("wr", [D + 1, D])
        gamma_b = sb("gamma_b", [P, D])
        beta_b = sb("beta_b", [P, D])
        dst_rel0 = sb("dst_rel0", [P, NB, TILES])
        dst_rel = sb("dst_rel", [P, NB, TILES])
        row_node = sb("row_node", [P, 1])
        base_i = sb("base_i", [1, NB], I32)
        passes_i = sb("passes_i", [1, 1], I32)
        orderly_i = sb("orderly_i", [1, 1], I32)
        h_flat = h_sb[:, :, :].rearrange("p t f -> p (t f)")
        taken = [0]

        def setup_only(columns):
            taken[0] += columns
            return h_flat[:, taken[0] - columns:taken[0]]
        rel_f = setup_only(4 * ROWS).rearrange("q (c e) -> q c e", c=4)
        dst_nat = setup_only(4 * ROWS).bitcast(I32).rearrange("q (c e) -> q c e", c=4)
        rel_nat = setup_only(2 * ROWS).bitcast(I16).rearrange("q (c e) -> q c e", c=4)
        diag_mn, diag_mx = setup_only(NB), setup_only(NB)
        base_r, span_r = setup_only(NB)[0:1, :], setup_only(NB)[0:1, :]
        col_mn, col_mx = setup_only(4), setup_only(4)
        span_m = setup_only(1)[0:1, :]
        due_i = setup_only(G * BPG)[0:1, :].bitcast(I32)
        early = setup_only(NB)[0:1, :]
        early_m = setup_only(1)[0:1, :]
        third = setup_only(1)
        iota_p = setup_only(1)
        iota_pi = setup_only(1).bitcast(I32)
        iota_i = setup_only(WIN).bitcast(I32)
        kvg = sb("kvg", [P, RING, TILES * KV])
        kv_slot = [kvg[:, k, :].rearrange("p (t f) -> p t f", f=KV) for k in range(RING)]
        h1_slot = [kvg[:, k, 0:TILES * (D + 1)].rearrange("p (t f) -> p t f", f=D + 1) for k in range(RING)]
        idx = sb("idx", [P, RING, TILES], I32)
        dst_row = sb("dst_row", [ROWS_W, RING, ROWS], I16)
        q_win = sb("q_win", [ROWS_W, RING, D], BF16)
        ea_t = sb("ea_t", [D + 1, RING, ROWS])
        sel = sb("sel", [P, 2, TILES, WIN])
        sel_t = sb("sel_t", [ROWS_W, 2, TILES, P], BF16)
        prod = sb("prod", [P, TILES * D])
        score = sb("score", [P, TILES * HEADS])
        msg = sb("msg", [P, 2, TILES, MSG])
        node_sum = sb("node_sum", [P, 2, TILES])
        node_sq = sb("node_sq", [P, 2, TILES])
        node_r = sb("node_r", [P, 2, TILES])
        centred = sb("centred", [P, 2, TILES, D])
        squares = msg[:, :, :, 0:D]
        normed = sb("normed", [P, 2, TILES, D])
        h_t = sb("h_t", [D + 1, 2, ROWS])
        kvq_out = sb("kvq_out", [P, 2, TILES, KVQ])
        q_out = sb("q_out", [P, 2, TILES, PARTS, D], BF16)
        q_rest = sb("q_rest", [P, 2, TILES, D])
        h_out = q_rest
        rz = sb("rz", [P, 2, TILES * HEADS])
        acc_stage = kvq_out[:, 0, :, :].rearrange("p t f -> p (t f)")[:, 0:ROWS]
        node_squares = kvq_out[:, 1, :, :].rearrange("p t f -> p (t f)")[:, 0:TILES * D].rearrange("p (t f) -> p t f", f=D)
        first_mean, mean_b, scale_b, shift_b, mean_sq = (sb(name, [P, D]) for name in (
            "first_mean", "mean_b", "scale_b", "shift_b", "mean_sq"))

        psum = ctx.enter_context(nc.psum_tensor("psum", [P, 8, 512], F32))
        bank = [psum[:, i, :] for i in range(8)]
        b_node, b_e, b_q, b_agg = bank[1], bank[2:4], bank[4:6], bank[6:8]
        b_own_t, b_neigh, b_own, b_first, b_sum, b_sum_sq = bank[0:6]
        node_banks = [psum[:, TILES * k:TILES * (k + 1), :] for k in range(2)]

        s_const = sem("s_const")
        s_x_first = sem("s_x_first")
        s_x = sem("s_x")
        s_dst_nat = sem("s_dst_nat")
        s_idx = [sem(f"s_idx{k}") for k in range(RING)]
        s_ea = [sem(f"s_ea{k}") for k in range(RING)]
        s_dstrow = [sem(f"s_dstrow{k}") for k in range(RING)]
        s_qwin = [sem(f"s_qwin{k}") for k in range(RING)]
        s_kv = [sem(f"s_kv{k}") for k in range(RING)]
        s_idx1 = [sem(f"s_idx1{k}") for k in range(RING)]
        s_h1g = [sem(f"s_h1g{k}") for k in range(RING)]
        s_gate = sem("s_gate")
        s_pool = sem("s_pool")
        s_iota = sem("s_iota")
        s_wq = sem("s_wq")
        s_wt = sem("s_wt")
        s_wt_sb = sem("s_wt_sb")
        s_place_step = sem("s_place_step")
        s_win_step = sem("s_win_step")
        s_rel_f = sem("s_rel_f")
        s_rel_t = sem("s_rel_t")
        s_rel_out = sem("s_rel_out")
        s_rel = sem("s_rel")
        s_relst = sem("s_relst")
        s_diag = sem("s_diag")
        s_bc = sem("s_bc")
        s_base = sem("s_base")
        s_sum_step = sem("s_sum_step")
        s_rstd_step = sem("s_rstd_step")
        s_cent = sem("s_cent")
        s_sq = sem("s_sq")
        s_sqsum = sem("s_sqsum")
        s_std = sem("s_std")
        s_normed = sem("s_normed")
        s_ht_ps = sem("s_ht_ps")
        s_ht = sem("s_ht")
        s_kvq = sem("s_kvq")
        s_kvq_out = sem("s_kvq_out")
        s_qhigh = sem("s_qhigh")
        s_qrest = sem("s_qrest")
        s_qmid = sem("s_qmid")
        s_qlow = sem("s_qlow")
        s_kvst = [sem(f"s_kvst{k}") for k in range(2)]
        s_qst = [sem(f"s_qst{k}") for k in range(2)]
        s_e = sem("s_e")
        s_q = sem("s_q")
        s_sel_t = sem("s_sel_t")
        s_kq = sem("s_kq")
        s_kqe = sem("s_kqe")
        s_dot = sem("s_dot")
        s_clip = sem("s_clip")
        s_exp = sem("s_exp")
        s_msg = sem("s_msg")
        s_agg = sem("s_agg")
        s_acc = sem("s_acc")
        s_pass = sem("s_pass")
        s_ones_col = sem("s_ones_col")
        s_mst = sem("s_mst")
        s_clear = sem("s_clear")
        s_mt = sem("s_mt")
        s_z_step = sem("s_z_step")
        s_hout = sem("s_hout")
        s_res = sem("s_res")
        s_msum_step = sem("s_msum_step")
        s_mcent = sem("s_mcent")
        s_msq_step = sem("s_msq_step")
        s_mstd = sem("s_mstd")
        s_mrstd = sem("s_mrstd")
        s_h1 = sem("s_h1")
        s_h1st = sem("s_h1st")
        s_acc0 = sem("s_acc0")
        s_sel1 = sem("s_sel1")
        s_agg1 = sem("s_agg1")
        s_acc1 = sem("s_acc1")
        s_pass1 = sem("s_pass1")
        s_zero_ps = sem("s_zero_ps")
        s_own_ld = sem("s_own_ld")
        s_own_ps = sem("s_own_ps")
        s_own_t = sem("s_own_t")
        s_fst = sem("s_fst")
        s_own_lin = sem("s_own_lin")
        s_lin = sem("s_lin")
        s_deg_step = sem("s_deg_step")
        s_neigh = sem("s_neigh")
        s_hh = sem("s_hh")
        s_first = sem("s_first")
        s_first_step = sem("s_first_step")
        s_hc = sem("s_hc")
        s_fsq = sem("s_fsq")
        s_stat = sem("s_stat")
        s_bn_step = sem("s_bn_step")
        s_var = sem("s_var")
        s_bstd = sem("s_bstd")
        s_shift = sem("s_shift")
        s_scaled = sem("s_scaled")
        s_shifted = sem("s_shifted")
        s_o = sem("s_o")
        s_out = sem("s_out")

        CONSTS = 13
        PADDED, IOTAS, IDENTITY, ONE, ONE_ROWS, CLEARED = 1, 4, 6, 9, 13, 14
        X_FIRST, X_LOADS = 7, 4

        def passes(eng):
            eng.wait_ge(s_base, 1)
            return eng.value_load(passes_i[0:1, 0:1], min_val=1, max_val=N // WIN + 1)

        def base_of(eng, b, w):
            first = eng.value_load(base_i[0:1, bass.ds(b, 1)], min_val=0, max_val=N - 1)
            node = first + w * WIN
            return (node + (node > N) * (N - node)).with_bounds(min_val=0, max_val=N)

        def orderly(eng):
            eng.wait_ge(s_base, 1)
            return eng.value_load(orderly_i[0:1, 0:1], min_val=0, max_val=1)

        def edge_steps(eng, w, step, in_order=None, midway=(), behind=()):
            def one(b, k, j):
                step(b, k, w * NB + b, w * RINGS + j,
                     isinstance(b, int) and b == 0, isinstance(b, int) and b == NB - 1, j)

            def rings(g, i0, i1):
                with eng.Fori(i0, i1) as i:
                    j = i + (g * STRIDE + 1)
                    for k in range(RING):
                        one(j * RING + k, k, j)

            def between(stages, g):
                due = [(late, fn) for late, fn in stages if not (isinstance(g, int) and g < late)]
                if due:
                    with eng.If(in_order == 1):
                        for late, fn in due:
                            fn(g - late)

            def group_rings(g):
                if any(not (isinstance(g, int) and g < late) for late, fn in midway):
                    rings(g, 0, STRIDE // 2)
                    between(midway, g)
                    rings(g, STRIDE // 2, STRIDE)
                else:
                    rings(g, 0, STRIDE)
                between(behind, g)
            latest = max([late for late, fn in list(midway) + list(behind)], default=0)
            for k in range(RING):
                one(k, k, 0)
            for g in range(latest):
                group_rings(g)
            with eng.Fori(latest, G - 1) as g:
                group_rings(g)
            between(midway, G - 1)
            for k in range(RING):
                one(LASTB + k, k, RINGS - 1)

        def other_groups(eng, in_order, stages, done=()):
            with eng.If(in_order == 0):
                with eng.Fori(0, G - 1) as g:
                    for left, fn in stages:
                        fn(g)
                for left, fn in stages:
                    if left < 0:
                        fn(G - 1)
            most = max(left for left, fn in stages)
            if most > 0:
                for left, fn in stages:
                    if left == 0:
                        fn(G - 1)
                with eng.If(in_order == 1):
                    for g in range(G - 1 - most, G - 1):
                        for left, fn in stages:
                            if g + left >= G - 1 and fn not in done:
                                fn(g)
            for left, fn in stages:
                if left > 0 or left == most == 0:
                    fn(G - 1)

        def added(g, turns):
            return turns * NB + 2 if turns is not None else g * BPG + (BPG + LATE + 2)

        def node_stages(eng, *stages, peel=2):
            depth = max(behind for behind, fn in stages)
            start = max(peel, depth + depth % 2)
            rounds = (G - start) // 2

            def apart(s):
                for behind, fn in stages:
                    if 0 <= s - behind < G:
                        fn(s - behind, (s - behind) % 2, (s - behind) // 2)
            for s in range(start):
                apart(s)
            with eng.Fori(0, rounds) as r:
                for s in (start, start + 1):
                    for behind, fn in stages:
                        fn(r * 2 + (s - behind), (s - behind) % 2, r + (s - behind) // 2)
            for s in range(start + 2 * rounds, G + depth):
                apart(s)

        def stores(k):
            return 16 * ((G + 1 - k) // 2 + 1)

        def used_rows(g, t):
            return min(max(N - g * ROWS - t * P, 0), P)

        def is_last(g):
            return isinstance(g, int) and g == G - 1

        def group(g):
            return bass.ds(g * TILES, TILES)

        block = ctx.enter_context(nc.Block())

        @block.sync
        def _(sp):
            for s, count in ((s_e, 2), (s_q, 2), (s_kq, RING), (s_kqe, 2), (s_msg, RING),
                             (s_agg, 2), (s_acc, 2), (s_agg1, RING), (s_acc1, 2), (s_sel1, 2),
                             (s_ht_ps, 2), (s_ht, 2), (s_kvq, 2), (s_kvq_out, 2), (s_qhigh, 2), (s_qrest, 2), (s_qlow, 2),
                             (s_kvst[0], 16), (s_kvst[1], 16), (s_qst[0], 16), (s_qst[1], 16),
                             (s_mt, 1), (s_hout, 1), (s_h1, 1), (s_h1st, 16),
                             (s_own_ps, 1), (s_own_t, 1), (s_own_lin, 1), (s_lin, 1), (s_hh, 1), (s_stat, 1)):
                sp.sem_inc(s, count)
            sp.dma_start(dst_nat[0:QCH, 0:3, :],
                         dst[0:3 * QCH * ROWS].rearrange("(c q e) -> q c e", c=3, e=ROWS)).then_inc(s_dst_nat, 16)
            sp.dma_start(dst_nat[0:WHOLE - 3 * QCH, 3, :],
                         dst[3 * QCH * ROWS:WHOLE * ROWS].rearrange("(q e) -> q e", e=ROWS)).then_inc(s_dst_nat, 16)
            for b in range(WHOLE, NB):
                sp.dma_start(dst_nat[b - 3 * QCH:b - 3 * QCH + 1, 3, :],
                             edges(dst, b).rearrange("(a e) -> a e", a=1)).then_inc(s_dst_nat, 16)
            tile_rows = lambda t0, t1: x[t0 * P:t1 * P, :].rearrange("(t p) f -> p t f", p=P)
            sp.dma_start(x_sb[:, 0:X_FIRST * TILES, :], tile_rows(0, X_FIRST * TILES)).then_inc(s_x_first, 16)
            row = lambda v: v.rearrange("(a d) -> a d", a=1)
            for to, of in ((wkvq[0:D, KV:KVQ], Wq), (wkvq[D:D + 1, KV:KVQ], row(bq)),
                           (wkvq[0:D, 0:D], Wk), (wkvq[0:D, D:KV], Wv), (wkvq[D:D + 1, 0:D], row(bk)),
                           (wkvq[D:D + 1, D:KV], row(bv)), (wl_in[:, :], Wl), (wr_in[:, :], Wr),
                           (we[0:D, :], We), (we[D:D + 1, :], row(be)),
                           (wr[D:D + 1, :], row(bl)), (gamma_b[:, :], row(gamma).to_broadcast([P, D])),
                           (beta_b[:, :], row(beta).to_broadcast([P, D]))):
                sp.dma_start(to, of).then_inc(s_const, 16)
            chunk = -(-(FULL - X_FIRST * TILES) // X_LOADS)
            for t0 in range(X_FIRST * TILES, FULL, chunk):
                t1 = min(t0 + chunk, FULL)
                sp.dma_start(x_sb[:, t0:t1, :], tile_rows(t0, t1)).then_inc(s_x, 16)
            sp.wait_ge(s_pool, PADDED)
            sp.dma_start(x_sb[0:REST, FULL, :], x[FULL * P:N, :]).then_inc(s_x, 16)
            sp.wait_ge(s_rel, 1)
            sp.dma_start(rel_tab.rearrange("(c q) e -> q c e", c=4), rel_nat[0:QCH, :, :]).then_inc(s_relst, 16)

            def store_kv(g, k, j):
                sp.wait_ge(s_kvq_out, g + 3)
                sp.dma_start(node_rows(kv_tab, g), kvq_out[:, k, :, 0:KV]).then_inc(s_kvst[k], 16)
            node_stages(sp, (0, store_kv))
            with sp.Fori(0, passes(sp)) as w:
                def load(b, k, n, turn, first, last, j):
                    for i in range(RING) if first else [0] if not isinstance(b, int) or b >= RING else []:
                        sp.wait_ge(s_kq, n + 1 + i)
                        if not only_repeats(b):
                            sp.dma_start(idx[:, k + i, :], edges(src, b + i)
                                         .rearrange("(p t) -> p t", t=TILES)).then_inc(s_idx[k + i], 16)
                    sp.wait_ge(s_msg, n + 1)
                    sp.dma_start(ea_t[0:D, k, :], edge_attr_t[:, bass.ds(start_of(b), ROWS)]).then_inc(s_ea[k], 16)
                    if first:
                        sp.wait_ge(s_relst, 16)
                        for i in range(2):
                            sp.wait_ge(s_qst[i], stores(i))
                    sp.dma_start(dst_row[:, k, :], rel_tab[bass.ds(b, 1), :]
                                 .to_broadcast([ROWS_W, ROWS])).then_inc(s_dstrow[k], 16)
                    sp.dma_start(q_win[:, k, :],
                                 q_tab[bass.ds(base_of(sp, b, w) * PARTS, ROWS_W), :]).then_inc(s_qwin[k], 16)
                edge_steps(sp, w, load)

            turns, in_order = passes(sp), orderly(sp)
            sp.wait_ge(s_msg, turns * NB + RING)
            sp.sem_inc(s_gate, 1)
            with sp.Fori(0, turns) as w:
                def load1(b, k, n, turn, first, last, j):
                    if only_repeats(b):
                        return
                    sp.wait_ge(s_agg1, n + 1)
                    sp.dma_start(idx[:, k, :], edges(src, b).rearrange("(p t) -> p t", t=TILES)).then_inc(s_idx1[k], 16)

                def load_own(g):
                    sp.wait_ge(s_h1st, 16 * (G + 1))
                    sp.wait_ge(s_own_ps, g + 1)
                    sp.sem_inc(s_gate, 1)
                    sp.dma_start(normed[:, 0, :, :], node_rows(h1_tab, g)).then_inc(s_own_ld, 16)
                edge_steps(sp, w, load1, in_order, midway=[(0, load_own)])
            other_groups(sp, in_order, [(-1, load_own)])

            def store_out(g, k, j):
                sp.wait_ge(s_o, g + 1)
                if is_last(g):
                    for t in range(TILES):
                        rows = used_rows(g, t)
                        if rows:
                            at = g * ROWS + t * P
                            sp.dma_start(out[at:at + rows, :], h_sb[0:rows, g * TILES + t, :]).then_inc(s_out, 16)
                else:
                    sp.dma_start(node_rows(out, g), h_sb[:, group(g), :]).then_inc(s_out, 16)
            node_stages(sp, (0, store_out))
            sp.wait_ge(s_out, 16 * (G - 1 + USED - (G - 1) * TILES))

        @block.gpsimd
        def _(pool):
            def made(ins, count=[0]):
                ins.then_inc(s_pool, 1)
                count[0] += 1
                pool.wait_ge(s_pool, count[0])

            made(pool.memset(x_sb[:, FULL:NT, :], 0.0))
            made(pool.iota(iota_i[:, :], pattern=[[1, WIN]], base=0, channel_multiplier=0))
            made(pool.iota(due_i, pattern=[[ROWS, G], [0, BPG]], base=0, channel_multiplier=0))
            made(pool.iota(iota_pi[:, :], pattern=[[0, 1]], base=0, channel_multiplier=1))
            made(pool.memset(ident[:, :], 0.0))
            made(pool.affine_select(out=ident[:, :], in_=ident[:, :], compare_op=ALU.not_equal, fill=1.0, base=0,
                                    pattern=[[-1, P]], channel_multiplier=1))
            made(pool.memset(ones[:, :], 1.0))
            made(pool.memset(eps[:, :], EPS))
            made(pool.memset(zero[:, :], 0.0))
            made(pool.memset(wl[:, :], 0.0))
            made(pool.memset(wl[D:D + 1, D:D + 1], 1.0))
            made(pool.memset(h_t[D:D + 1, :, :], 1.0))
            made(pool.memset(ea_t[D:D + 1, :, :], 1.0))
            made(pool.memset(acc[:, :], 0.0))

            def third_part(g, k, j):
                if is_last(g):
                    return
                pool.wait_ge(s_qmid, g + 1)
                pool.sem_inc(s_gate, 1)
                pool.tensor_tensor(q_out[:, k, :, 2, :], q_rest[:, k, :, :], q_out[:, k, :, 1, :],
                                   ALU.subtract).then_inc(s_qlow, 1)
            node_stages(pool, (0, third_part))

            for k in range(2):
                pool.wait_ge(s_kvst[k], stores(k))
            with pool.Fori(0, passes(pool)) as w:
                def gather(b, k, n, turn, first, last, j):
                    if only_repeats(b):
                        return
                    pool.wait_ge(s_idx[k], gathers(k, w, j) * 16)
                    pool.sem_inc(s_gate, 1)
                    pool.wait_ge(s_msg, n + 1)
                    pool.sem_inc(s_gate, 1)
                    for t in range(TILES):
                        pool.indirect_dma_start(
                            out=kv_slot[k][:, t, :], out_offset=None, in_=kv_tab[:, :],
                            in_offset=bass.IndirectOffsetOnAxis(ap=idx[:, k, t:t + 1], axis=0)).then_inc(s_kv[k], 16)
                edge_steps(pool, w, gather)

            pool.wait_ge(s_acc0, 1)
            for k in range(RING):
                pool.memset(h1_slot[k][:, :, D:D + 1], 1.0).then_inc(s_ones_col, 1)
                pool.wait_ge(s_ones_col, k + 1)
            pool.wait_ge(s_h1st, 16 * (G + 1))
            with pool.Fori(0, passes(pool)) as w:
                def gather1(b, k, n, turn, first, last, j):
                    if only_repeats(b):
                        return
                    pool.wait_ge(s_idx1[k], gathers(k, w, j) * 16)
                    pool.sem_inc(s_gate, 1)
                    for t in range(TILES):
                        pool.indirect_dma_start(
                            out=h1_slot[k][:, t, 0:D], out_offset=None, in_=h1_tab[:, :],
                            in_offset=bass.IndirectOffsetOnAxis(ap=idx[:, k, t:t + 1], axis=0)).then_inc(s_h1g[k], 16)
                edge_steps(pool, w, gather1)

            pool.wait_ge(s_shift, 1)
            def shift(g, k, j):
                rows = h_sb[:, group(g), :]
                pool.wait_ge(s_scaled, g + 1)
                pool.sem_inc(s_gate, 1)
                pool.tensor_tensor(rows, rows, shift_b[:, :].unsqueeze(1).to_broadcast([P, TILES, D]),
                                   ALU.add).then_inc(s_shifted, 1)
            node_stages(pool, (0, shift))

        @block.tensor
        def _(pe):
            pe.wait_ge(s_pool, ONE_ROWS)
            pe.wait_ge(s_diag, 8)
            for c in range(4):
                part = slice(c * QCH, (c + 1) * QCH)
                pe.matmul(bank[2][0:1, part], ones[0:QCH, 0:1], diag_mn[0:QCH, part], start=True, stop=True)
                mm = pe.matmul(bank[3][0:1, part], ones[0:QCH, 0:1], diag_mx[0:QCH, part], start=True, stop=True)
            mm.then_inc(s_bc, 1)
            pe.wait_ge(s_rel_f, 4)
            for c in range(4):
                turned = rel_f[0:QCH, c, :].rearrange("q (p t) -> q t p", t=TILES)
                for t in range(TILES):
                    mm = pe.transpose(bank[4 + c][:, t * QCH:(t + 1) * QCH], turned[:, t, :], ident[0:QCH, 0:QCH])
            mm.then_inc(s_rel_t, 1)
            pe.wait_ge(s_const, 16 * CONSTS)
            pe.transpose(bank[0][0:D, 0:D], wl_in[:, :], ident[0:D, 0:D])
            pe.transpose(bank[0][0:D, P:P + D], wr_in[:, :], ident[0:D, 0:D]).then_inc(s_wt, 1)

            def turn_normed(g, k, j):
                pe.wait_ge(s_normed, g + 1)
                pe.wait_ge(s_kvq_out, g + 1)
                for t in range(TILES):
                    mm = pe.transpose(node_banks[k][0:D, t, KVQ:KVQ + P], normed[:, k, t, :], ident[:, :])
                mm.then_inc(s_ht_ps, 1)

            def project(k, tiles):
                for t in tiles:
                    mm = pe.matmul(node_banks[k][:, t, 0:KVQ], h_t[:, k, t * P:(t + 1) * P], wkvq[:, :],
                                   start=True, stop=True)
                return mm

            def project_most(g, k, j):
                pe.wait_ge(s_ht, g + 3)
                project(k, range(TILES - 1))

            def project_last(g, k, j):
                project(k, [TILES - 1]).then_inc(s_kvq, 1)
            pe.wait_ge(s_wt_sb, 1)
            pe.wait_ge(s_wq, 1)
            pe.wait_ge(s_base, 1)
            pe.wait_ge(s_rel_out, 4)
            node_stages(pe, (3, project_most), (2, turn_normed), (3, project_last))

            pe.wait_ge(s_kvq_out, G + 2)
            turns, in_order = passes(pe), orderly(pe)

            def turn_sums(g):
                pe.wait_ge(s_mst, g + 1)
                pe.wait_ge(s_hout, g + 1)
                for t in range(TILES):
                    mm = pe.transpose(b_node[:, t * MSG:(t + 1) * MSG], acc_stage[0:MSG, t * P:(t + 1) * P],
                                      ident[0:MSG, 0:MSG])
                mm.then_inc(s_mt, 1)

            with pe.Fori(0, turns) as w:
                def aggregate(k, n):
                    pe.wait_ge(s_msg, n + 1 + RING)
                    pe.wait_ge(s_acc, n + 1)
                    for t in range(TILES):
                        mm = pe.matmul(b_agg[k % 2][0:MSG, 0:WIN], msg[:, k % 2, t, :], sel[:, k % 2, t, :],
                                       start=(t == 0), stop=(t == TILES - 1))
                    mm.then_inc(s_agg, 1)

                def step(b, k, n, turn, first, last, j):
                    edge = ea_t[:, k, :].rearrange("c (p t) -> c t p", t=TILES)
                    pe.wait_ge(s_ea[k], (turn + 1) * 16)
                    pe.wait_ge(s_kqe, n + 1)
                    for t in range(TILES):
                        mm = pe.matmul(b_e[k % 2][:, t * D:(t + 1) * D], edge[:, t, :], we[:, :],
                                       start=True, stop=True)
                    mm.then_inc(s_e, 1)
                    pe.wait_ge(s_qwin[k], (turn + 1) * 16)
                    pe.wait_ge(s_sel_t, n + 1)
                    pe.wait_ge(s_kq, n + RING - 1)
                    for t in range(TILES):
                        mm = pe.matmul(b_q[k % 2][:, t * D:(t + 1) * D], sel_t[:, k % 2, t, :], q_win[:, k, :],
                                       start=True, stop=True)
                    mm.then_inc(s_q, 1)
                    if not first:
                        aggregate((k - 1) % RING, n - 1)
                    if last:
                        aggregate(k, n)
                edge_steps(pe, w, step, in_order, midway=[(1, turn_sums)])
            other_groups(pe, in_order, [(0, turn_sums)])

            def own_product(g):
                pe.wait_ge(s_own_ld, g * 16 + 16)
                pe.wait_ge(s_own_t, g + 1)
                for t in range(TILES):
                    mm = pe.transpose(b_own_t[0:D, t * P:(t + 1) * P], normed[:, 0, t, :], ident[:, :])
                mm.then_inc(s_own_ps, 1)
                pe.wait_ge(s_own_t, g + 2)
                pe.wait_ge(s_hh, g + 1)
                for t in range(TILES):
                    mm = pe.matmul(b_own[:, t * D:(t + 1) * D], h_t[:, 0, t * P:(t + 1) * P], wr[:, :],
                                   start=True, stop=True)
                mm.then_inc(s_own_lin, 1)

            def neighbour_product(g):
                pe.wait_ge(s_fst, g + 1)
                pe.wait_ge(s_hh, g + 1)
                for t in range(TILES):
                    mm = pe.matmul(b_neigh[:, t * (D + 1):(t + 1) * (D + 1)], acc_stage[0:D + 1, t * P:(t + 1) * P], wl[:, :],
                                   start=True, stop=True)
                mm.then_inc(s_lin, 1)
                if not is_last(g):
                    with pe.If(g == 0):
                        pe.wait_ge(s_hh, 2)
                        pe.matmul(b_first[:, 0:TILES * D], ones[:, :], h_sb[:, group(0), :], start=True,
                                  stop=True).then_inc(s_first, 1)

            def sum_group(g):
                pe.wait_ge(s_hc, g + 1)
                pe.wait_ge(s_fsq, g + 1)
                if is_last(g):
                    for t in range(TILES):
                        rows = used_rows(g, t)
                        if rows:
                            at = slice(t * D, (t + 1) * D)
                            pe.matmul(b_sum[:, at], ones[0:rows, :], h_sb[0:rows, g * TILES + t, :],
                                      start=False, stop=True, skip_group_check=True)
                            mm = pe.matmul(b_sum_sq[:, at], ones[0:rows, :], node_squares[0:rows, t, :],
                                           start=False, stop=True, skip_group_check=True)
                else:
                    pe.matmul(b_sum[:, 0:TILES * D], ones[:, :], h_sb[:, group(g), :],
                              start=False, stop=False, skip_group_check=True)
                    mm = pe.matmul(b_sum_sq[:, 0:TILES * D], ones[:, :], node_squares, start=False, stop=False,
                                   skip_group_check=True)
                mm.then_inc(s_stat, 1)

            pe.wait_ge(s_ones_col, RING)
            pe.wait_ge(s_zero_ps, 1)
            with pe.Fori(0, turns) as w:
                def step1(b, k, n, turn, first, last, j):
                    if not only_repeats(b):
                        pe.wait_ge(s_h1g[k], gathers(k, w, j) * (16 * TILES))
                    pe.wait_ge(s_sel1, n + 3)
                    pe.wait_ge(s_acc1, n + 1)
                    for t in range(TILES):
                        mm = pe.matmul(b_agg[k % 2][0:D + 1, 0:WIN], h1_slot[k][:, t, :], sel[:, k % 2, t, :],
                                       start=(t == 0), stop=(t == TILES - 1))
                    mm.then_inc(s_agg1, 1)
                edge_steps(pe, w, step1, in_order, midway=[(0, own_product)], behind=[(0, neighbour_product), (1, sum_group)])
            other_groups(pe, in_order, [(-1, own_product), (0, neighbour_product), (1, sum_group)])

        @block.scalar
        def _(act):
            def deviation(k):
                return nc.scalar.activation(node_sq[:, k, :], node_sq[:, k, :], ACT.Sqrt, bias=eps[:, 0:1], scale=1.0 / D)

            act.wait_ge(s_const, 16 * CONSTS)
            nc.scalar.mul(wkvq[:, KV:KVQ], wkvq[:, KV:KVQ], float(DH) ** -0.5).then_inc(s_wq, 1)
            act.wait_ge(s_rel_t, 1)
            for c in range(4):
                nc.scalar.copy(dst_rel0[:, c * QCH:(c + 1) * QCH, :].rearrange("p q t -> p t q"),
                               bank[4 + c][:, 0:TILES * QCH].rearrange("p (t q) -> p t q", t=TILES)).then_inc(s_rel_out, 1)
            act.wait_ge(s_pool, ONE)

            def root(g, k, j):
                act.wait_ge(s_sqsum, g + 1)
                deviation(k).then_inc(s_std, 1)

            def rows_out(g, k, j):
                act.wait_ge(s_kvq, g + 3)
                act.wait_ge(s_kvst[k], (j + 1) * 16)
                act.wait_ge(s_qrest, g + 1)
                nc.scalar.copy(kvq_out[:, k, :, :], node_banks[k][:, :, 0:KVQ]).then_inc(s_kvq_out, 1)

            def square(g, k, j):
                act.wait_ge(s_cent, g + 1)
                nc.scalar.activation(squares[:, k, :, :], centred[:, k, :, :], ACT.Square).then_inc(s_sq, 1)

            def cut_off(g, k, j):
                act.wait_ge(s_ht_ps, g + 3)
                act.wait_ge(s_kvq, g + 1)
                nc.scalar.activation(h_t[0:D, k, :].rearrange("f (t p) -> f t p", p=P),
                                     node_banks[k][0:D, :, KVQ:KVQ + P], ACT.Relu).then_inc(s_ht, 1)

            def second_part(g, k, j):
                act.wait_ge(s_qrest, g + 3)
                nc.scalar.copy(q_out[:, k, :, 1, :], q_rest[:, k, :, :]).then_inc(s_qmid, 1)

            def store_q(g, k, j):
                act.wait_ge(s_qlow, g + 3)
                nc.scalar.dma_start(q_tab[bass.ds(g * ROWS * PARTS, ROWS * PARTS), :]
                                    .rearrange("(t p s) f -> p t (s f)", p=P, s=PARTS),
                                    q_out[:, k, :, :, :].rearrange("p t s f -> p t (s f)")).then_inc(s_qst[k], 16)
            node_stages(act, (2, cut_off), (1, root), (3, rows_out), (5, store_q), (0, square), (4, second_part))

            turns, in_order = passes(act), orderly(act)

            def stage_sums(g, turns=None):
                columns = acc[:, bass.ds(g * ROWS, ROWS)]
                act.wait_ge(s_acc, added(g, turns))
                act.wait_ge(s_mt, g + 1)
                act.sem_inc(s_gate, 1)
                nc.scalar.copy(acc_stage[0:MSG, :], columns).then_inc(s_mst, 1)
                act.wait_ge(s_mst, g + 1)
                act.sem_inc(s_gate, 1)
                nc.scalar.copy(columns, zero[0:MSG, :].to_broadcast([MSG, ROWS])).then_inc(s_clear, 1)

            def normalise(g):
                act.wait_ge(s_msq_step, g * 2 + 2)
                deviation(0).then_inc(s_mstd, 1)
                act.wait_ge(s_mrstd, g + 1)
                act.wait_ge(s_h1st, g * 16 + 16)
                for t in range(TILES):
                    made = nc.scalar.activation(normed[:, 0, t, :], centred[:, 0, t, :], ACT.Relu, scale=node_r[:, 0, t:t + 1])
                made.then_inc(s_h1, 1)
                act.wait_ge(s_h1, g + 2)
                nc.scalar.dma_start(node_rows(h1_tab, g), normed[:, 0, :, :]).then_inc(s_h1st, 16)

            with act.Fori(0, turns) as w:
                def step(b, k, n, turn, first, last, j):
                    act.wait_ge(s_clip, n + 1)
                    act.wait_ge(s_agg, n + 1)
                    nc.scalar.activation(msg[:, k % 2, :, D:MSG], score[:, :].rearrange("p (t h) -> p t h", h=HEADS),
                                         ACT.Exp).then_inc(s_exp, 1)
                edge_steps(act, w, step, in_order, midway=[(2, normalise)], behind=[(0, stage_sums)])
            other_groups(act, in_order, [(0, lambda g: stage_sums(g, turns)), (1, normalise)])

            def own_transposed(g):
                act.wait_ge(s_own_ps, g + 2)
                act.wait_ge(s_own_lin, g + 1)
                nc.scalar.copy(h_t[0:D, 0, :], b_own_t[0:D, :]).then_inc(s_own_t, 1)

            def stage_and_square(g, turns=None):
                act.wait_ge(s_acc1, added(g, turns))
                act.wait_ge(s_lin, g + 1)
                act.sem_inc(s_gate, 1)
                nc.scalar.copy(acc_stage[0:D + 1, :], acc[0:D + 1, bass.ds(g * ROWS, ROWS)]).then_inc(s_fst, 1)
                act.wait_ge(s_hc, g + 1)
                act.wait_ge(s_stat, g + 1)
                act.sem_inc(s_gate, 1)
                nc.scalar.activation(node_squares, h_sb[:, group(g), :], ACT.Square).then_inc(s_fsq, 1)
            with act.Fori(0, turns) as w:
                edge_steps(act, w, lambda b, k, n, turn, first, last, j: None, in_order,
                           midway=[(0, own_transposed)], behind=[(0, stage_and_square)])
            other_groups(act, in_order, [(-1, own_transposed), (0, lambda g: stage_and_square(g, turns))])
            act.wait_ge(s_var, 1)
            nc.scalar.activation(scale_b[:, :], scale_b[:, :], ACT.Sqrt, bias=eps[:, 0:1]).then_inc(s_bstd, 1)

        @block.vector
        def _(dve):
            def per_node(v):
                return v.unsqueeze(2).to_broadcast([P, TILES, D])

            def per_feature(v):
                return v.unsqueeze(1).to_broadcast([P, TILES, D])

            def counted(s_step, before):
                count = [0]

                def step(ins):
                    count[0] += 1
                    ins.then_inc(s_step, 1)
                    dve.wait_ge(s_step, before + count[0])
                return step

            def spread(rows, k, own_step, done):
                own_step(nc.vector.reduce_sum(node_sum[:, k, :], rows, AX_X))
                dve.sem_inc(s_gate, 1)
                nc.vector.scalar_tensor_tensor(out=centred[:, k, :, :], in0=per_node(node_sum[:, k, :]), scalar=-1.0 / D,
                                               in1=rows, op0=ALU.mult, op1=ALU.add).then_inc(done, 1)

            step = counted(s_win_step, 0)
            dve.wait_ge(s_dst_nat, 16 * (2 + NB - WHOLE))
            step(nc.vector.tensor_reduce(col_mn[0:QCH, :], dst_nat[0:QCH, :, :], AX_X, ALU.min))
            step(nc.vector.tensor_reduce(col_mx[0:QCH, :], dst_nat[0:QCH, :, :], AX_X, ALU.max))
            dve.wait_ge(s_pool, IDENTITY)
            for c in range(4):
                for diag, col in ((diag_mn, col_mn), (diag_mx, col_mx)):
                    nc.vector.tensor_scalar(diag[0:QCH, c * QCH:(c + 1) * QCH], ident[0:QCH, 0:QCH], col[0:QCH, c:c + 1],
                                            None, ALU.mult).then_inc(s_diag, 1)
            for c in range(4):
                nc.vector.tensor_scalar(rel_f[0:QCH, c, :], dst_nat[0:QCH, c, :], col_mn[0:QCH, c:c + 1],
                                        None, ALU.subtract).then_inc(s_rel_f, 1)
            dve.wait_ge(s_rel_f, 4)
            nc.vector.tensor_copy(rel_nat[0:QCH, :, :], rel_f[0:QCH, :, :]).then_inc(s_rel, 1)
            step(nc.vector.tensor_copy(iota_p, iota_pi))
            step(nc.vector.tensor_scalar(third, iota_p, (PARTS - 1) / 2.0, 1.0 / PARTS, ALU.subtract, ALU.mult))
            step(nc.vector.tensor_scalar(third, third, ROUND, None, ALU.add))
            step(nc.vector.tensor_scalar(row_node[:, :], third, ROUND, -float(WIN), ALU.subtract, ALU.add))
            nc.vector.tensor_copy(iota_w[:, :], iota_i[:, :])
            dve.wait_ge(s_bc, 1)
            step(nc.vector.tensor_copy(base_r, bank[2][0:1, 0:NB]))
            step(nc.vector.tensor_tensor(span_r, bank[3][0:1, 0:NB], base_r, ALU.subtract))
            step(nc.vector.tensor_reduce(span_m, span_r, AX_X, ALU.max))
            step(nc.vector.tensor_scalar(span_m, span_m, (WIN - 1) / 2.0, 1.0 / WIN, ALU.subtract, ALU.mult))
            step(nc.vector.tensor_scalar(span_m, span_m, ROUND, None, ALU.add))
            step(nc.vector.tensor_scalar(span_m, span_m, ROUND, 1.0, ALU.subtract, ALU.add))
            step(nc.vector.tensor_copy(passes_i[0:1, :], span_m))
            step(nc.vector.tensor_tensor(early[:, LATE:NB], due_i[:, 0:NB - LATE], base_r[:, LATE:NB], ALU.is_gt))
            step(nc.vector.tensor_reduce(early_m, early[:, LATE:NB], AX_X, ALU.max))
            step(nc.vector.tensor_tensor(early_m, early_m, span_m, ALU.add))
            nc.vector.tensor_scalar(orderly_i[0:1, :], early_m, 1.0, None, ALU.is_equal)
            nc.vector.tensor_copy(base_i[0:1, :], base_r).then_inc(s_base, 1)
            dve.wait_ge(s_wt, 1)
            dve.wait_ge(s_pool, ONE_ROWS)
            nc.vector.tensor_copy(wl[0:D, 0:D], bank[0][0:D, 0:D])
            nc.vector.tensor_copy(wr[0:D, :], bank[0][0:D, P:P + D]).then_inc(s_wt_sb, 1)

            def sum_squares(g, k, j):
                dve.wait_ge(s_sq, g + 1)
                nc.vector.reduce_sum(node_sq[:, k, :], squares[:, k, :, :], AX_X).then_inc(s_sqsum, 1)

            def sum_features(g, k, j):
                if isinstance(g, int) and g == 0:
                    dve.wait_ge(s_x_first, 16)
                if isinstance(g, int) and g == X_FIRST:
                    dve.wait_ge(s_x, 16 * (X_LOADS + 1))
                nc.vector.reduce_sum(node_sum[:, k, :], x_sb[:, group(g), :], AX_X).then_inc(s_sum_step, 1)

            def centre(g, k, j):
                dve.wait_ge(s_sum_step, g + 1)
                dve.sem_inc(s_gate, 1)
                nc.vector.scalar_tensor_tensor(out=centred[:, k, :, :], in0=per_node(node_sum[:, k, :]), scalar=-1.0 / D,
                                               in1=x_sb[:, group(g), :], op0=ALU.mult, op1=ALU.add).then_inc(s_cent, 1)

            def factors_of(g, k, j):
                dve.wait_ge(s_std, g + 1)
                nc.vector.reciprocal(node_r[:, k, :], node_sq[:, k, :]).then_inc(s_rstd_step, 1)

            def scale(g, k, j):
                dve.wait_ge(s_rstd_step, g + 1)
                dve.wait_ge(s_ht_ps, g + 1)
                nc.vector.tensor_tensor(normed[:, k, :, :], centred[:, k, :, :], per_node(node_r[:, k, :]),
                                        ALU.mult).then_inc(s_normed, 1)

            def first_of_q(g, k, j):
                dve.wait_ge(s_kvq_out, g + 3)
                dve.wait_ge(s_qst[k], (j + 1) * 16)
                dve.sem_inc(s_gate, 1)
                nc.vector.tensor_copy(q_out[:, k, :, 0, :], kvq_out[:, k, :, KV:KVQ]).then_inc(s_qhigh, 1)

            def rest_of_q(g, k, j):
                dve.wait_ge(s_qhigh, g + 3)
                dve.wait_ge(s_qlow, g + 1)
                nc.vector.tensor_tensor(q_rest[:, k, :, :], kvq_out[:, k, :, KV:KVQ], q_out[:, k, :, 0, :],
                                        ALU.subtract).then_inc(s_qrest, 1)
            node_stages(dve, (2, scale), (0, sum_features), (1, sum_squares), (0, centre), (4, first_of_q), (1, factors_of), (4, rest_of_q),
                        peel=X_FIRST + 1)

            last, k = G - 1, (G - 1) % 2
            dve.wait_ge(s_qmid, last + 1)
            nc.vector.tensor_tensor(q_out[:, k, :, 2, :], q_rest[:, k, :, :], q_out[:, k, :, 1, :],
                                    ALU.subtract).then_inc(s_qlow, 1)

            dve.wait_ge(s_rel_out, 4)
            step = counted(s_place_step, 0)
            for b in range(WHOLE, NB):
                rep = repeated_partitions(b)
                if rep:
                    step(nc.vector.memset(dst_rel0[0:rep, b, :], -1.0 - WIN))

            def place_windows():
                return nc.vector.tensor_scalar(dst_rel[:, :, :], dst_rel0[:, :, :], float(WIN), None, ALU.add)
            step(place_windows())

            def move_windows(done, w, turned):
                nc.vector.tensor_scalar(dst_rel[:, :, :], dst_rel[:, :, :], float(WIN), None,
                                        ALU.subtract).then_inc(done, 1)
                if turned:
                    nc.vector.tensor_scalar(row_node[:, :], row_node[:, :], float(WIN), None, ALU.add).then_inc(done, 1)
                dve.wait_ge(done, (w + 1) * (2 if turned else 1))

            def select(b, k):
                return nc.vector.tensor_tensor(
                    sel[:, k % 2, :, :], iota_w[:, :].unsqueeze(1).to_broadcast([P, TILES, WIN]),
                    dst_rel[:, bass.ds(b, 1), :].rearrange("p a t -> p (a t)").unsqueeze(2).to_broadcast([P, TILES, WIN]),
                    ALU.is_equal)

            def add_sums(b, k, w, n, rows, s_from, credit, s_done):
                at = acc[0:rows, bass.ds(base_of(dve, b, w), WIN)]
                dve.wait_ge(s_from, n + 1 + credit)
                dve.wait_ge(s_done, n + 2)
                dve.sem_inc(s_gate, 1)
                nc.vector.tensor_tensor(at, at, b_agg[k % 2][0:rows, 0:WIN], ALU.add).then_inc(s_done, 1)

            dve.wait_ge(s_pool, CLEARED)
            turns, in_order = passes(dve), orderly(dve)

            def add_means(g):
                sums = b_node[:, 0:TILES * MSG].rearrange("p (t f) -> p t f", f=MSG)
                z = rz[:, 0, :].rearrange("p (t h) -> p t h", h=HEADS)
                heads = lambda v: v.rearrange("p t (h d) -> p t h d", h=HEADS)
                rows = x_sb[:, group(g), :]
                own_step = counted(s_z_step, g * 2)
                dve.wait_ge(s_mt, g + 2)
                own_step(nc.vector.tensor_scalar(z, sums[:, :, D:MSG], Z_EPS, None, ALU.add))
                own_step(nc.vector.reciprocal(z, z))
                nc.vector.tensor_tensor(heads(h_out[:, 0, :, :]), heads(sums[:, :, 0:D]),
                                        z.unsqueeze(3).to_broadcast([P, TILES, HEADS, DH]), ALU.mult).then_inc(s_hout, 1)
                dve.wait_ge(s_hout, g + 2)
                dve.sem_inc(s_gate, 1)
                nc.vector.tensor_tensor(rows, rows, h_out[:, 0, :, :], ALU.add).then_inc(s_res, 1)

            def centre1(g):
                rows = x_sb[:, group(g), :]
                dve.wait_ge(s_res, g + 1)
                dve.wait_ge(s_h1, g + 1)
                dve.sem_inc(s_gate, 1)
                spread(rows, 0, counted(s_msum_step, g), s_mcent)
                dve.wait_ge(s_mcent, g + 1)
                own_step = counted(s_msq_step, g * 2)
                own_step(nc.vector.tensor_tensor(node_squares, centred[:, 0, :, :], centred[:, 0, :, :], ALU.mult))
                nc.vector.reduce_sum(node_sq[:, 0, :], node_squares, AX_X).then_inc(s_msq_step, 1)

            def factors(g):
                dve.wait_ge(s_mstd, g + 1)
                nc.vector.reciprocal(node_r[:, 0, :], node_sq[:, 0, :]).then_inc(s_mrstd, 1)

            with dve.Fori(0, turns) as w:
                move_windows(s_pass, w, True)

                def select_t(b, k, n, turn):
                    dve.wait_ge(s_dstrow[k], (turn + 1) * 16)
                    dve.wait_ge(s_q, n + 1)
                    nc.vector.tensor_scalar(sel_t[:, k % 2, :, :], dst_row[:, k, :].rearrange("w (p t) -> w t p", t=TILES),
                                            row_node[0:ROWS_W, 0:1], None, ALU.is_equal).then_inc(s_sel_t, 1)

                def step(b, k, n, turn, first, last, j):
                    if first:
                        select_t(b, k, n, turn)
                    heads = lambda v: v.rearrange("p t (h d) -> p t h d", h=HEADS)
                    p3 = prod[:, :].rearrange("p (t f) -> p t f", f=D)
                    if not only_repeats(b):
                        dve.wait_ge(s_kv[k], gathers(k, w, j) * (16 * TILES))
                    dve.wait_ge(s_q, n + 3)
                    nc.vector.tensor_tensor(p3, kv_slot[k][:, :, 0:D], b_q[k % 2][:, 0:TILES * D]
                                            .rearrange("p (t f) -> p t f", f=D), ALU.mult).then_inc(s_kq, 1)
                    if not last:
                        select_t(b + 1, (k + 1) % RING, n + 1, turn + (k + 1) // RING)
                    dve.wait_ge(s_e, n + 3)
                    dve.wait_ge(s_kq, n + 1 + RING)
                    nc.vector.tensor_tensor(prod[:, :], prod[:, :], b_e[k % 2][:, 0:TILES * D], ALU.mult).then_inc(s_kqe, 1)
                    dve.wait_ge(s_agg, n + 1)
                    dve.sem_inc(s_gate, 1)
                    select(b, k)
                    dve.wait_ge(s_kqe, n + 3)
                    nc.vector.reduce_sum(score[:, :], prod[:, :].rearrange("p (g d) -> p g d", d=DH), AX_X).then_inc(s_dot, 1)
                    if not first:
                        add_sums(b - 1, (k - 1) % RING, w, n - 1, MSG, s_agg, 2, s_acc)
                    dve.wait_ge(s_dot, n + 1)
                    nc.vector.tensor_scalar(score[:, :], score[:, :], -CLIP, CLIP, ALU.max, ALU.min).then_inc(s_clip, 1)
                    dve.wait_ge(s_exp, n + 1)
                    nc.vector.tensor_tensor(heads(msg[:, k % 2, :, 0:D]), heads(kv_slot[k][:, :, D:KV]),
                                            msg[:, k % 2, :, D:MSG].unsqueeze(3).to_broadcast([P, TILES, HEADS, DH]),
                                            ALU.mult).then_inc(s_msg, 1)
                    if last:
                        add_sums(b, k, w, n, MSG, s_agg, 2, s_acc)
                edge_steps(dve, w, step, in_order, midway=[(1, add_means), (2, factors)], behind=[(1, centre1)])
            dve.wait_ge(s_acc, turns * NB + 2)
            dve.sem_inc(s_gate, 1)
            with dve.If(in_order == 1):
                centre1(G - 2)
            place_windows().then_inc(s_acc0, 1)
            other_groups(dve, in_order, [(0, add_means), (1, centre1), (1, factors)], done=[centre1])

            def second_layer(g):
                rows = h_sb[:, group(g), :]
                products = b_neigh[:, 0:TILES * (D + 1)].rearrange("p (t f) -> p t f", f=D + 1)
                own_step = counted(s_deg_step, g * 2)
                dve.wait_ge(s_lin, g + 2)
                own_step(nc.vector.tensor_scalar(node_sum[:, 0, :].unsqueeze(2), products[:, :, D:D + 1], 1.0, None, ALU.max))
                own_step(nc.vector.reciprocal(node_r[:, 0, :], node_sum[:, 0, :]))
                nc.vector.tensor_tensor(centred[:, 0, :, :], products[:, :, 0:D], per_node(node_r[:, 0, :]),
                                        ALU.mult).then_inc(s_neigh, 1)
                dve.wait_ge(s_neigh, g + 1)
                dve.sem_inc(s_gate, 1)
                nc.vector.tensor_tensor(rows, b_own[:, 0:TILES * D].rearrange("p (t f) -> p t f", f=D), centred[:, 0, :, :],
                                        ALU.add).then_inc(s_hh, 1)
                if not is_last(g):
                    with dve.If(g == 0):
                        first_step = counted(s_first_step, 0)
                        dve.wait_ge(s_first, 1)
                        first_step(nc.vector.reduce_sum(first_mean[:, :], over_tiles(b_first), AX_X))
                        first_step(nc.vector.tensor_scalar(first_mean[:, :], first_mean[:, :], 1.0 / ROWS, None, ALU.mult))
                dve.wait_ge(s_hh, g + 2)
                dve.sem_inc(s_gate, 1)
                nc.vector.tensor_tensor(rows, rows, per_feature(first_mean[:, :]), ALU.subtract).then_inc(s_hc, 1)

            def over_tiles(sums):
                return sums[:, 0:TILES * D].rearrange("p (t f) -> p f t", f=D)
            nc.vector.memset(b_sum[:, 0:TILES * D], 0.0)
            nc.vector.memset(b_sum_sq[:, 0:TILES * D], 0.0).then_inc(s_zero_ps, 1)
            dve.wait_ge(s_clear, G)
            with dve.Fori(0, turns) as w:
                move_windows(s_pass1, w, False)

                def step1(b, k, n, turn, first, last, j):
                    dve.wait_ge(s_agg1, n + 3)
                    dve.sem_inc(s_gate, 1)
                    select(b, k).then_inc(s_sel1, 1)
                    if not first:
                        add_sums(b - 1, (k - 1) % RING, w, n - 1, D + 1, s_agg1, RING, s_acc1)
                    if last:
                        add_sums(b, k, w, n, D + 1, s_agg1, RING, s_acc1)
                edge_steps(dve, w, step1, in_order, behind=[(0, second_layer)])
            other_groups(dve, in_order, [(0, second_layer)])

            step = counted(s_bn_step, 0)
            dve.wait_ge(s_stat, G + 1)
            nc.vector.reduce_sum(mean_b[:, :], over_tiles(b_sum), AX_X)
            step(nc.vector.reduce_sum(scale_b[:, :], over_tiles(b_sum_sq), AX_X))
            step(nc.vector.tensor_scalar(mean_b[:, :], mean_b[:, :], 1.0 / N, None, ALU.mult))
            step(nc.vector.tensor_tensor(mean_sq[:, :], mean_b[:, :], mean_b[:, :], ALU.mult))
            nc.vector.scalar_tensor_tensor(out=scale_b[:, :], in0=scale_b[:, :], scalar=1.0 / N, in1=mean_sq[:, :],
                                           op0=ALU.mult, op1=ALU.subtract).then_inc(s_var, 1)
            dve.wait_ge(s_const, 16 * CONSTS)
            dve.wait_ge(s_bstd, 1)
            step(nc.vector.reciprocal(scale_b[:, :], scale_b[:, :]))
            step(nc.vector.tensor_tensor(scale_b[:, :], scale_b[:, :], gamma_b[:, :], ALU.mult))
            step(nc.vector.tensor_tensor(mean_b[:, :], mean_b[:, :], scale_b[:, :], ALU.mult))
            nc.vector.tensor_tensor(shift_b[:, :], beta_b[:, :], mean_b[:, :], ALU.subtract).then_inc(s_shift, 1)

            def scale_h(g, k, j):
                rows = h_sb[:, group(g), :]
                nc.vector.tensor_tensor(rows, rows, per_feature(scale_b[:, :]), ALU.mult).then_inc(s_scaled, 1)

            def finish(g, k, j):
                rows = h_sb[:, group(g), :]
                dve.wait_ge(s_shifted, g + 1)
                dve.sem_inc(s_gate, 1)
                nc.vector.scalar_tensor_tensor(out=rows, in0=rows, scalar=0.0, in1=x_sb[:, group(g), :],
                                               op0=ALU.max, op1=ALU.add).then_inc(s_o, 1)
            node_stages(dve, (0, scale_h), (2, finish))


_INS = ['x', 'src', 'dst', 'edge_attr_96', 'L0_gnn_Wq', 'L0_gnn_bq', 'L0_gnn_Wk', 'L0_gnn_bk', 'L0_gnn_We', 'L0_gnn_be',
        'L0_gnn_Wv', 'L0_gnn_bv', 'L1_gnn_Wl', 'L1_gnn_bl', 'L1_gnn_Wr', 'L1_gnn_gamma', 'L1_gnn_beta']


def kernel(**inputs):
    import numpy as _np
    import concourse.bacc as _bacc
    from concourse import mybir as _mybir
    from concourse.bass_utils import run_bass_kernel_spmd as _run

    nc = _bacc.Bacc("TRN2", target_bir_lowering=False, num_devices=1)
    arrays, args = {}, []
    for name in _INS:
        a = _np.asarray(inputs[name])
        a = _np.ascontiguousarray(a.T if name == 'edge_attr_96' else a)
        arrays[f"in_{name}_dram"] = a
        args.append(nc.dram_tensor(f"in_{name}_dram", a.shape, _mybir.dt.from_np(a.dtype), kind="ExternalInput").ap())
    out = nc.dram_tensor("out_0_dram", arrays["in_x_dram"].shape, _mybir.dt.float32, kind="ExternalOutput").ap()
    graph_attention_then_sage_kernel(nc, *args, out)
    r = _run(nc, [arrays], core_ids=[0])
    return r.results[0]["out_0_dram"]
```
